# Optimizing a Trainium2 kernel written in Bass

```python
import numpy as np
import jax
import jax.numpy as jnp

def _softmax(x, axis=-1):
    return jax.nn.softmax(x, axis=axis)

def _gelu(x):
    return jax.nn.gelu(x, approximate=True)

def _silu(x):
    return jax.nn.silu(x)

def _sigmoid(x):
    return jax.nn.sigmoid(x)

def _layernorm(x, axis=-1, eps=1e-05):
    m = jnp.mean(x, axis=axis, keepdims=True)
    v = jnp.var(x, axis=axis, keepdims=True)
    return (x - m) / jnp.sqrt(v + eps)

def _scatter_add(tgt, idx, src, axis=0):
    return tgt.at[idx].add(src)

def _segment_sum(src, seg, n):
    return jax.ops.segment_sum(src, seg, n)
kernel_name = 'mk_gnn_resnorm_d1_gnn_r8_cabb2d'

def setup_inputs(seed: int=0):
    np.random.seed(seed)
    _w = jnp.asarray

    def _rec_inputs():
        import jax
        import jax.numpy as jnp
        _gk = jax.random.key(seed)
        x = -0.0005121 + 1.001 * jax.random.normal(jax.random.fold_in(_gk, 1), (6250, 160), jnp.float32)
        _s = jax.random.randint(jax.random.fold_in(_gk, 2), (100000,), 0, 6250, jnp.int32)
        _d = jax.random.randint(jax.random.fold_in(_gk, 3), (100000,), 0, 6250, jnp.int32)
        _loop = jnp.arange(6250, dtype=jnp.int32)
        src = jnp.concatenate([_s, _d, _loop])
        dst = jnp.concatenate([_d, _s, _loop])
        _o = jnp.argsort(dst, stable=True)
        src = src[_o]
        dst = dst[_o]
        edge_attr_4 = 0.000735704 + 1.0001 * jax.random.normal(jax.random.fold_in(_gk, 11), (206250, 4), jnp.float32)
        node_vec1 = -0.00719938 + 0.999885 * jax.random.normal(jax.random.fold_in(_gk, 13), (6250, 1), jnp.float32)
        return (x, src, dst, edge_attr_4, node_vec1)
    x, src, dst, edge_attr_4, node_vec1 = _rec_inputs()

    def _L0_gnn_setup():
        import jax, jax.numpy as jnp
        import numpy as np
        N = 2500
        E = 80000
        INV_SQRT3 = 0.5773502691896258
        INV8 = 0.125
        INV_SQRT32 = 0.17677669529663687
        INV64 = 0.015625
        INV32 = 0.03125
        INV_SQRT2048 = 0.022097086912079608
        key = jax.random.key(seed)
        ks = jax.random.split(key, 16)
        f32 = jnp.float32
        return {'node_features': jax.random.normal(ks[0], (N, 160), f32), 'edge_index': jax.random.randint(ks[1], (2, E), 0, N), 'edge_attr_tensor': jax.random.normal(ks[2], (E, 4), f32), 'node_attr_scalar_raw': jax.random.normal(ks[3], (N, 1), f32), 'Wm_ss': jax.random.normal(ks[4], (64, 64), f32), 'Wm_vv': jax.random.normal(ks[5], (32, 64), f32), 'Wm_sv': jax.random.normal(ks[6], (64, 32), f32), 'Wm_vs': jax.random.normal(ks[7], (32, 32), f32), 'Lm_s': jax.random.normal(ks[8], (64, 64), f32), 'Lm_v': jax.random.normal(ks[9], (32, 32), f32), 'Wu_ss': jax.random.normal(ks[10], (64, 64, 64), f32), 'Wu_vv': jax.random.normal(ks[11], (32, 32, 64), f32), 'Wu_sv': jax.random.normal(ks[12], (64, 32, 32), f32), 'Wu_vs': jax.random.normal(ks[13], (32, 64, 32), f32), 'Lu_s': jax.random.normal(ks[14], (64, 64), f32), 'Lu_v': jax.random.normal(ks[15], (32, 32), f32)}
    _L0_gnn_all = _L0_gnn_setup()
    _L0_gnn_in = {k: v for k, v in _L0_gnn_all.items() if k in ('Wm_ss', 'Wm_vv', 'Wm_sv', 'Wm_vs', 'Lm_s', 'Lm_v', 'Wu_ss', 'Wu_vv', 'Wu_sv', 'Wu_vs', 'Lu_s', 'Lu_v')}
    del _L0_gnn_all
    return {'x': x, 'src': src, 'dst': dst, 'edge_attr_4': edge_attr_4, 'node_vec1': node_vec1, 'L0_gnn_Wm_ss': _L0_gnn_in['Wm_ss'], 'L0_gnn_Wm_vv': _L0_gnn_in['Wm_vv'], 'L0_gnn_Wm_sv': _L0_gnn_in['Wm_sv'], 'L0_gnn_Wm_vs': _L0_gnn_in['Wm_vs'], 'L0_gnn_Lm_s': _L0_gnn_in['Lm_s'], 'L0_gnn_Lm_v': _L0_gnn_in['Lm_v'], 'L0_gnn_Wu_ss': _L0_gnn_in['Wu_ss'], 'L0_gnn_Wu_vv': _L0_gnn_in['Wu_vv'], 'L0_gnn_Wu_sv': _L0_gnn_in['Wu_sv'], 'L0_gnn_Wu_vs': _L0_gnn_in['Wu_vs'], 'L0_gnn_Lu_s': _L0_gnn_in['Lu_s'], 'L0_gnn_Lu_v': _L0_gnn_in['Lu_v']}

def reference(x, src, dst, edge_attr_4, node_vec1, L0_gnn_Wm_ss, L0_gnn_Wm_vv, L0_gnn_Wm_sv, L0_gnn_Wm_vs, L0_gnn_Lm_s, L0_gnn_Lm_v, L0_gnn_Wu_ss, L0_gnn_Wu_vv, L0_gnn_Wu_sv, L0_gnn_Wu_vs, L0_gnn_Lu_s, L0_gnn_Lu_v):
    import jax
    import jax.numpy as jnp

    def _L0_gnn_ref(node_features, edge_index, edge_attr_tensor, node_attr_scalar_raw, Wm_ss, Wm_vv, Wm_sv, Wm_vs, Lm_s, Lm_v, Wu_ss, Wu_vv, Wu_sv, Wu_vs, Lu_s, Lu_v):
        import jax, jax.numpy as jnp
        import numpy as np
        N = 2500
        E = 80000
        INV_SQRT3 = 0.5773502691896258
        INV8 = 0.125
        INV_SQRT32 = 0.17677669529663687
        INV64 = 0.015625
        INV32 = 0.03125
        INV_SQRT2048 = 0.022097086912079608
        n = node_features.shape[0]
        e = edge_attr_tensor.shape[0]
        row, col = (edge_index[0], edge_index[1])
        r_vec = edge_attr_tensor[:, :3]
        dist = edge_attr_tensor[:, 3:4]
        xj = node_features[col]
        s = xj[:, :64]
        v = xj[:, 64:].reshape(e, 32, 3)
        m0 = s @ Wm_ss * dist * INV8 + jnp.einsum('eui,ei->eu', v, r_vec) @ Wm_vv * (INV_SQRT3 * INV_SQRT32)
        m1 = (s @ Wm_sv)[:, :, None] * r_vec[:, None, :] * INV8 + jnp.einsum('eui,uw->ewi', v, Wm_vs) * dist[:, :, None] * INV_SQRT32
        m0 = m0 + s @ Lm_s * INV8
        m1 = m1 + jnp.einsum('eui,uw->ewi', v, Lm_v) * INV_SQRT32
        msg = jnp.concatenate([m0, m1.reshape(e, 96)], axis=-1)
        agg = jax.ops.segment_sum(msg, row, num_segments=n)
        a0 = agg[:, :64]
        a1 = agg[:, 64:].reshape(n, 32, 3)
        xs = node_features[:, :64]
        xv = node_features[:, 64:].reshape(n, 32, 3)
        u0 = jnp.einsum('nu,nv,uvw->nw', xs, a0, Wu_ss) * INV64 + jnp.einsum('nui,nvi,uvw->nw', xv, a1, Wu_vv) * (INV_SQRT3 * INV32)
        u1 = jnp.einsum('nu,nvi,uvw->nwi', xs, a1, Wu_sv) * INV_SQRT2048 + jnp.einsum('nui,nv,uvw->nwi', xv, a0, Wu_vs) * INV_SQRT2048
        u0 = u0 + xs @ Lu_s * INV8
        u1 = u1 + jnp.einsum('nui,uw->nwi', xv, Lu_v) * INV_SQRT32
        upd = jnp.concatenate([u0, u1.reshape(n, 96)], axis=-1)
        return node_features + upd
    edge_index = jnp.stack([src, dst])
    x = _layernorm(x + _L0_gnn_ref(x, edge_index, edge_attr_4, node_vec1, L0_gnn_Wm_ss, L0_gnn_Wm_vv, L0_gnn_Wm_sv, L0_gnn_Wm_vs, L0_gnn_Lm_s, L0_gnn_Lm_v, L0_gnn_Wu_ss, L0_gnn_Wu_vv, L0_gnn_Wu_sv, L0_gnn_Wu_vs, L0_gnn_Lu_s, L0_gnn_Lu_v), axis=-1)
    return x

_drawn_inputs = setup_inputs


def setup_inputs(seed=0):
    import zlib

    import numpy as np

    out = dict(_drawn_inputs(seed))
    spreads = {}
    factors = {}
    for name, (base, spread) in spreads.items():
        noise = np.random.default_rng([zlib.crc32(name.encode()), seed]).standard_normal(out[name].shape)
        drawn = base * np.exp(spread * noise) if base else spread * noise
        out[name] = jnp.asarray(drawn.astype(out[name].dtype))
    for name, factor in factors.items():
        out[name] = (out[name] * factor).astype(out[name].dtype)
    return out
```

```python
from contextlib import ExitStack

import concourse.bass as bass
from concourse import mybir

P = 128
LANE = 4
SUPER = P * LANE
SHIFT = SUPER.bit_length() - 1
BITS = P.bit_length() - 1
STEP = 13
FIRST_STEPS = (4, 12)
CHUNK_STEPS = 27
REC = 6
RING = 4
S, V = 64, 32
D = S + 3 * V
SR, VR = 2 * D, 2 * D + 3 * S
SUMS = VR + V
SUMS_A = 2 * D
BANK = 512
ZSS, ZU = S * S // BANK, V * V // BANK
ZALL = ZSS + 2 * ZU
ZRING = 4
RED = ZSS + ZU - 1
REGION = 16592
EPS = 1e-5
INV_SQRT3, INV8, INV_SQRT32 = 0.5773502691896258, 0.125, 0.17677669529663687
INV64, INV32, INV_SQRT2048 = 0.015625, 0.03125, 0.022097086912079608

ALU = mybir.AluOpType
ACT = mybir.ActivationFunctionType
F32, BF16 = mybir.dt.float32, mybir.dt.bfloat16
I32, U32, U16 = mybir.dt.int32, mybir.dt.uint32, mybir.dt.uint16
AX_X = mybir.AxisListType.X
ds = bass.ds


def spread(ap, axis, n):
    ap = ap.unsqueeze(axis)
    shape = list(ap.shape)
    shape[axis] = n
    return ap.to_broadcast(shape)


def gnn_kernel(nc, x, src, dst, attr, node_vec, Wm_ss, Wm_vv, Wm_sv, Wm_vs, Lm_s, Lm_v,
               Wu_ss, Wu_vv, Wu_sv, Wu_vs, Lu_s, Lu_v, out):
    N, E = x.shape[0], src.shape[0]
    NB = -(-N // P)
    NK = NB + 1 + (NB + 1) % 2
    NU = NB + NB % 2
    NX = NU + 1
    NTAIL = N - (NB - 1) * P
    STEPS = -(-(-(-E // P)) // STEP)
    STEPS += STEPS % 2
    COLS = STEPS * STEP
    CHUNK = CHUNK_STEPS * STEP
    chunks = []
    while not chunks or sum(chunks[-1]) < STEPS:
        at = sum(chunks[-1]) if chunks else 0
        n = FIRST_STEPS[len(chunks)] if len(chunks) < len(FIRST_STEPS) else CHUNK_STEPS
        chunks.append((at, min(n, STEPS - at)))
    FULL = E // COLS
    REST = E - FULL * COLS
    assert FULL == P - 1 and 0 < REST < COLS and NX <= NK + 1
    GROUPS = -(-(P * COLS // SUPER + NK) // RING) * RING
    assert GROUPS <= BANK
    SLOTS = GROUPS * SUPER

    table = nc.dram_tensor("edge_table", (SLOTS, REC), F32, kind="Internal").ap()
    groups_of_table = table.rearrange("(q p j) w -> q p (j w)", p=P, j=LANE)

    ctx = ExitStack()
    with ctx:
        def sb(name, shape, dt=F32):
            return ctx.enter_context(nc.sbuf_tensor(name, shape, dt))

        def sem(name):
            return ctx.enter_context(nc.semaphore(name))

        xall = sb("xall", [P, NX, D])
        sums = sb("sums", [P, NK + 1, SUMS])
        ident = sb("ident", [P, P])
        iota = sb("iota", [P, P])
        group_bucket = sb("group_bucket", [P, GROUPS], I32)
        region = sb("region", [P, REGION])

        place = [0]

        def carve(shape, dt=F32):
            n = 1
            for d in shape:
                n *= d
            words = n if dt in (F32, I32, U32) else -(-n // 2)
            v = region[:, place[0]:place[0] + words]
            place[0] += -(-words // 8) * 8
            assert place[0] <= REGION, place[0]
            if dt is not F32:
                v = v.bitcast(dt)[:, 0:n]
            if len(shape) == 2:
                v = v.rearrange("p (a b) -> p a b", b=shape[1])
            if len(shape) == 3:
                v = v.rearrange("p (a b c) -> p a b c", b=shape[1], c=shape[2])
            return v

        row_i = carve([COLS], I32)
        col_i = carve([COLS], I32)
        attr_s = carve([COLS, 4])
        block_b = carve([COLS], BF16)
        slot = carve([COLS])
        ones_row = carve([CHUNK])
        same = [carve([CHUNK], U16) for _ in range(2)]
        scan = [carve([CHUNK]) for _ in range(2)]
        junk = slot.bitcast(BF16)[:, 0:COLS]
        FILL = GROUPS // 4 * LANE // 4
        empty = carve([FILL, REC])
        bucket_no = carve([NK])
        count = carve([NK])
        total_i = carve([NK], I32)
        groups_f = carve([NK])
        first_group = carve([NK])
        before = carve([NK])
        ones_mat = carve([P])
        lower = carve([P])
        first_col = carve([1])
        group_no = carve([GROUPS])
        started = carve([GROUPS])
        stage_rec = [carve([STEP, REC]) for _ in range(2)]
        stage_slot = [carve([STEP], I32) for _ in range(2)]

        place[0] = 0
        rec = [carve([LANE, REC]) for _ in range(RING)]
        xx = [carve([LANE, 2 * D]) for _ in range(RING)]
        xr = [carve([LANE, 3 * S + V]) for _ in range(RING)]
        hot = [carve([LANE, P]) for _ in range(RING)]
        vprod = [carve([LANE, 3 * V]) for _ in range(RING)]

        place[0] = 0
        w_ss = carve([S * S // 2])
        w_u1 = carve([V * V])
        w_vv = carve([V * V // P, S])
        w_msg = [carve([D]) for _ in range(6)]
        w_lin = [carve([D]) for _ in range(2)]
        blk_sum = carve([SUMS])
        blk_x = [carve([D]) for _ in range(2)]
        flip = [carve([2 * BANK]) for _ in range(2)]
        agg = [carve([D]) for _ in range(2)]
        a0_t = [carve([P]) for _ in range(2)]
        gram = carve([V * V])
        gram_t = [carve([BANK]) for _ in range(2)]
        gtmp = carve([V * V])
        rr = [carve([D]) for _ in range(2)]
        y1 = [carve([D]) for _ in range(2)]
        y2 = carve([D])
        stats = carve([6])
        moments = carve([2])
        std = carve([1])
        rstd = carve([1])
        at = place[0]
        prod_ss = [carve([BANK]) for _ in range(2)]
        prod_u = carve([3 * (BANK // V) * 2 * V])
        place[0] = at
        raw_ss = carve([S * S // 2])
        raw_u1 = carve([V * V])

        psum = ctx.enter_context(nc.psum_tensor("psum", [P, 8, BANK], F32))

        s_passed = sem("wait_passed")
        s_pad = sem("edge_pads_cleared")
        s_edges = sem("edges_loaded")
        s_attr = sem("attributes_loaded")
        s_x = sem("x_loaded")
        s_const = sem("constants_ready")
        s_empty = sem("empty_records_ready")
        s_table = sem("table_cleared")
        s_v = sem("vector_chain")
        s_count = sem("edges_counted")
        s_prefix = sem("prefixes_ready")
        s_start = sem("group_starts_ready")
        s_startT = sem("group_starts_turned")
        s_began = sem("started_ready")
        s_gb = sem("group_buckets_summed")
        s_slots = sem("slots_ready")
        s_scan = sem("scan_chain")
        s_staged = sem("records_staged")
        s_scattered = [sem(f"records_scattered{h}") for h in range(2)]
        s_sums0 = sem("sums_cleared")
        s_rec = [sem(f"records_loaded{r}") for r in range(RING)]
        s_xg = [sem(f"x_gathered{r}") for r in range(RING)]
        s_xd = sem("x_times_dist_ready")
        s_vp = sem("v_products_ready")
        s_xr = sem("edge_features_ready")
        s_grp = sem("group_summed")
        s_free = sem("group_buffers_free")
        s_w = sem("weights_cleared")
        s_wload = sem("weights_loaded")
        s_wready = sem("weights_ready")
        s_blk = sem("block_staged")
        s_t = sem("block_turned")
        s_tt = sem("turned_block_copied")
        s_ag = sem("messages_summed")
        s_agc = sem("messages_copied")
        s_a0 = sem("a0_turned")
        s_a0c = sem("a0_turned_copied")
        s_z = sem("product_bank_ready")
        s_zfree = sem("product_banks_free")
        s_red = sem("products_reduced")
        s_g = sem("gram_chain")
        s_gt = sem("gram_turned")
        s_gtc = sem("gram_turned_copied")
        s_u = sem("update_summed")
        s_main = sem("block_products_done")
        s_y = sem("norm_chain")
        s_var = sem("variance_ready")
        s_std = sem("deviation_ready")
        s_done = sem("block_done")
        s_store = sem("stored")

        CONSTS = 8

        block = ctx.enter_context(nc.Block())

        def weight_loads():
            for h in range(2):
                yield raw_ss[h * S:h * S + S, :].rearrange("p (v w) -> p v w", v=S), Wu_ss[:, :, h * V:h * V + V]
            yield raw_u1[0:S, :], Wu_sv.rearrange("u v w -> u (v w)")
            yield raw_u1[S:P, :].rearrange("p (u w) -> p u w", w=V), Wu_vs.rearrange("u v w -> v u w")
            yield w_vv, Wu_vv.rearrange("u v w -> (u v) w").rearrange("(c p) w -> p c w", p=P)
            yield w_msg[0][0:S, 0:S], Lm_s
            yield w_msg[2][0:S, 0:S], Wm_ss
            for i in range(2):
                yield w_msg[4][S * i:S * i + S, S + V * i:S + V * i + V], Wm_sv
            yield w_msg[5][0:S, S + 2 * V:D], Wm_sv
            yield w_msg[5][S:S + V, 0:S], Wm_vv
            yield w_lin[0][0:S, 0:S], Lu_s
            for i in range(3):
                c = slice(S + V * i, S + V * i + V)
                yield w_msg[1][i:3 * V:3, c], Lm_v
                yield w_msg[3][i:3 * V:3, c], Wm_vs
                yield w_lin[1][i:3 * V:3, c], Lu_v

        WLOADS = len(list(weight_loads()))

        @block.sync
        def _(sp):
            for s in (s_count, s_scan, s_gt, s_gtc, s_main, s_done):
                sp.sem_inc(s, 1)
            sp.wait_ge(s_pad, 1)
            for tile_, dram in ((row_i, src), (col_i, dst)):
                sp.dma_start(tile_[0:FULL, :], dram[0:FULL * COLS].rearrange("(p t) -> p t", t=COLS)).then_inc(s_edges, 16)
                sp.dma_start(tile_[FULL:P, 0:REST], dram[FULL * COLS:E].rearrange("(p t) -> p t", p=1)).then_inc(s_edges, 16)
            sp.dma_start(attr_s[0:FULL, :, :], attr[0:FULL * COLS, :].rearrange("(p t) w -> p t w", t=COLS)).then_inc(s_attr, 16)
            sp.dma_start(attr_s[FULL:P, 0:REST, :], attr[FULL * COLS:E, :].rearrange("(p t) w -> p t w", p=1)).then_inc(s_attr, 16)
            sp.wait_ge(s_empty, 3)
            rows = SLOTS // P
            flat = table.rearrange("(p r) w -> p r w", r=rows)
            for c in range(rows // FILL):
                sp.dma_start(flat[:, c * FILL:(c + 1) * FILL, :], empty).then_inc(s_table, 16)
            sp.wait_ge(s_const, CONSTS)
            sp.dma_start(xall[:, 0:NB - 1, :], x[0:(NB - 1) * P, :].rearrange("(b p) d -> p b d", p=P)).then_inc(s_x, 16)
            sp.dma_start(xall[0:NTAIL, NB - 1, :], x[(NB - 1) * P:N, :]).then_inc(s_x, 16)

            for h in range(2):
                sp.wait_ge(s_scattered[h], 16 * STEP * (STEPS // 2))
            with sp.Fori(0, GROUPS // RING) as i:
                for r in range(RING):
                    sp.wait_ge(s_free, i * RING + r + 1)
                    sp.dma_start(rec[r].rearrange("p j w -> p (j w)"),
                                 groups_of_table[ds(i * RING + r, 1)].rearrange("q p f -> (q p) f")).then_inc(s_rec[r], 16)

            sp.wait_ge(s_w, 1)
            with nc.allow_non_contiguous_dma(reason="small weights"):
                for to, frm in weight_loads():
                    sp.dma_start(to, frm).then_inc(s_wload, 16)
            pairs = NU // 2
            with sp.Fori(0, pairs - 1) as i:
                sp.wait_ge(s_done, 2 * i + 3)
                sp.dma_start(out[ds(i * 2 * P, 2 * P), :].rearrange("(b p) d -> p b d", p=P),
                             xall[:, ds(i * 2, 2), :]).then_inc(s_store, 16)
            sp.wait_ge(s_done, NU + 1)
            stores = pairs - 1
            for b in range(NU - 2, NB):
                n = min(P, N - b * P)
                sp.dma_start(out[b * P:b * P + n, :], xall[0:n, b, :]).then_inc(s_store, 16)
                stores += 1
            sp.wait_ge(s_store, 16 * stores)

        @block.gpsimd
        def _(pool):
            g = nc.gpsimd
            g.iota(iota[:, :], [[1, P]], base=0, channel_multiplier=0, allow_small_or_imprecise_dtypes=True).then_inc(s_const, 1)
            g.iota(bucket_no, [[1, NK]], base=0, channel_multiplier=0, allow_small_or_imprecise_dtypes=True).then_inc(s_const, 1)
            g.iota(group_no, [[1, GROUPS]], base=0, channel_multiplier=0, allow_small_or_imprecise_dtypes=True).then_inc(s_const, 1)
            g.memset(ones_mat, 1.0).then_inc(s_const, 1)
            g.memset(ones_row, 1.0).then_inc(s_const, 1)
            pool.wait_ge(s_const, 5)
            g.affine_select(out=lower, in_=ones_mat, pattern=[[1, P]], compare_op=ALU.is_gt, fill=0.0,
                            base=0, channel_multiplier=-1).then_inc(s_const, 1)
            g.affine_select(out=ident[:, :], in_=ones_mat, pattern=[[1, P]], compare_op=ALU.is_equal, fill=0.0,
                            base=0, channel_multiplier=-1).then_inc(s_const, 1)
            g.memset(xall[:, NB - 1:NX, :], 0.0).then_inc(s_const, 1)
            pool.wait_ge(s_table, 16 * (SLOTS // P // FILL))
            with pool.Fori(0, STEPS // 2) as i:
                for h in range(2):
                    pool.wait_ge(s_staged, i * 2 + h + 1)
                    pool.sem_inc(s_passed, 1)
                    for j in range(STEP):
                        g.indirect_dma_start(
                            out=table, out_offset=bass.IndirectOffsetOnAxis(ap=stage_slot[h][:, j:j + 1].bitcast(U32), axis=0),
                            in_=stage_rec[h][:, j, :], in_offset=None).then_inc(s_scattered[h], 16)
            with pool.Fori(0, GROUPS // RING) as i:
                for r in range(RING):
                    pool.wait_ge(s_rec[r], i * 16 + 16)
                    pool.sem_inc(s_passed, 1)
                    for j in range(LANE):
                        g.indirect_dma_start(
                            out=xx[r][:, j, 0:D], out_offset=None, in_=x,
                            in_offset=bass.IndirectOffsetOnAxis(ap=rec[r][:, j, 4:5].bitcast(U32), axis=0)).then_inc(s_xg[r], 16)
            with pool.Fori(0, NU // 2) as i:
                for p in range(2):
                    pool.wait_ge(s_agc, i * 2 + p + 1)
                    pool.wait_ge(s_gt, i * 4 + 2 * p + 1)
                    xv = blk_x[p][:, S:D].rearrange("p (u i) -> p u i", i=3)
                    a1 = agg[p][:, S:D].rearrange("p (i v) -> p i v", i=3)
                    gm, gt = gram.rearrange("p (u v) -> p u v", v=V), gtmp.rearrange("p (u v) -> p u v", v=V)
                    n = i * 10 + p * 5
                    for c in range(3):
                        to = gt if c else gm
                        if c == 2:
                            pool.wait_ge(s_g, n + 3)
                        g.tensor_tensor(to, spread(xv[:, :, c], 2, V), spread(a1[:, c, :], 1, V), ALU.mult).then_inc(s_g, 1)
                        if c:
                            pool.wait_ge(s_g, n + 2 * c)
                            g.tensor_tensor(gm, gm, gt, ALU.add).then_inc(s_g, 1)

        @block.scalar
        def _(act):
            a = nc.scalar
            act.wait_ge(s_attr, 32)
            act.wait_ge(s_edges, 64)
            def stage(i):
                for h in range(2):
                    cols = ds(i * 2 * STEP + h * STEP, STEP)
                    act.wait_ge(s_slots, i * 2 + h + 1)
                    if type(i) is not int:
                        act.wait_ge(s_scattered[h], i * 16 * STEP)
                    a.activation(stage_rec[h][:, :, 0:4], attr_s[:, cols, :], ACT.Copy)
                    a.activation(stage_rec[h][:, :, 4].bitcast(I32), col_i[:, cols], ACT.Copy)
                    a.activation(stage_rec[h][:, :, 5], row_i[:, cols], ACT.Copy)
                    a.activation(stage_slot[h], slot[:, cols], ACT.Copy).then_inc(s_staged, 1)

            stage(0)
            with act.Fori(1, STEPS // 2) as i:
                stage(i)
            with act.Fori(0, GROUPS // RING) as i:
                for r in range(RING):
                    act.wait_ge(s_xg[r], i * 16 * LANE + 16 * LANE)
                    for j in range(LANE):
                        last = a.activation(xx[r][:, j, D:2 * D], xx[r][:, j, 0:D], ACT.Copy, scale=rec[r][:, j, 3:4])
                    last.then_inc(s_xd, 1)

            act.wait_ge(s_wload, 16 * WLOADS)
            a.activation(w_ss.rearrange("p (w v) -> p w v", v=S), raw_ss.rearrange("p (v w) -> p w v", w=V), ACT.Copy, scale=INV64)
            a.activation(w_u1.rearrange("p (w v) -> p w v", v=V), raw_u1.rearrange("p (v w) -> p w v", w=V), ACT.Copy,
                         scale=INV_SQRT2048)
            a.activation(w_vv, w_vv, ACT.Copy, scale=INV_SQRT3 * INV32)
            for k, rows, factor in ((0, slice(0, S), INV8), (1, slice(0, 3 * V), INV_SQRT32), (2, slice(0, S), INV8),
                                    (3, slice(0, 3 * V), INV_SQRT32), (4, slice(0, P), INV8), (5, slice(0, S), INV8),
                                    (5, slice(S, S + V), INV_SQRT3 * INV_SQRT32)):
                a.activation(w_msg[k][rows, :], w_msg[k][rows, :], ACT.Copy, scale=factor)
            a.activation(w_lin[0][0:S, :], w_lin[0][0:S, :], ACT.Copy, scale=INV8)
            a.activation(w_lin[1][0:3 * V, :], w_lin[1][0:3 * V, :], ACT.Copy, scale=INV_SQRT32).then_inc(s_wready, 1)
            act.wait_ge(s_x, 32)

            def ahead(b, p, first=False):
                if not (first and type(b) is int and b == 0):
                    act.wait_ge(s_main, b)
                act.wait_ge(s_t, b)
                a.activation(blk_sum, sums[:, ds(b, 1), :].rearrange("p o c -> p (o c)"), ACT.Copy)
                a.activation(blk_x[p], xall[:, ds(b, 1), :].rearrange("p o c -> p (o c)"), ACT.Copy).then_inc(s_blk, 1)
                act.wait_ge(s_t, b + 1)
                a.activation(flip[p][0:S, 0:3 * P], psum[0:S, 4, 0:3 * P], ACT.Copy)
                a.activation(flip[p][S:P, 2 * P:3 * P], psum[0:S, 4, 2 * P:3 * P], ACT.Copy)
                a.activation(flip[p][:, 3 * P:BANK], psum[:, 4, 3 * P:BANK], ACT.Copy)
                a.activation(flip[p][0:3 * V, BANK:2 * BANK], psum[0:3 * V, 5, :], ACT.Copy).then_inc(s_tt, 1)
                act.wait_ge(s_ag, b + 1)
                a.activation(agg[p], psum[:, 6, 0:D], ACT.Copy).then_inc(s_agc, 1)
                if not first:
                    deviation(b - 2)
                act.wait_ge(s_a0, b + 1)
                a.activation(a0_t[p][S:P, :], psum[0:S, 6, 256:256 + P], ACT.Copy).then_inc(s_a0c, 1)

            def deviation(b):
                act.wait_ge(s_var, b + 1)
                a.activation(std, moments[:, 1:2], ACT.Sqrt).then_inc(s_std, 1)

            ahead(0, 0, True)

            def gram_pair(i, start):
                for p in range(2):
                    b = i * 2 + p
                    ahead(b + 1, 1 - p, start and p == 0)
                    for h in range(2):
                        act.wait_ge(s_gt, b * 2 + h + 2)
                        a.activation(gram_t[h], psum[:, 4 + h, :], ACT.Copy).then_inc(s_gtc, 1)

            gram_pair(0, True)
            with act.Fori(1, NU // 2) as i:
                gram_pair(i, False)
            deviation(NU - 1)

        @block.vector
        def _(dve):
            v = nc.vector
            for t, w in ((row_i, NB * P), (col_i, 0)):
                last = v.memset(t[:, REST:COLS], w)
            v.memset(attr_s[:, REST:COLS, :], 0.0).then_inc(s_pad, 1)
            v.memset(empty, 0.0).then_inc(s_empty, 1)
            dve.wait_ge(s_empty, 1)
            v.memset(empty[:, :, 5], -1.0).then_inc(s_empty, 2)
            dve.wait_ge(s_edges, 64)
            v.tensor_scalar(slot.bitcast(I32), row_i, BITS, None, ALU.arith_shift_right).then_inc(s_v, 1)
            dve.wait_ge(s_v, 1)
            v.tensor_copy(block_b, slot.bitcast(I32)).then_inc(s_v, 1)
            v.tensor_scalar(row_i, row_i, P - 1, None, ALU.bitwise_and).then_inc(s_v, 1)
            dve.wait_ge(s_v, 3)
            dve.wait_ge(s_const, CONSTS)
            with dve.Fori(0, NK) as k:
                dve.wait_ge(s_count, k + 1)
                v.tensor_scalar(junk, block_b, bucket_no[:, ds(k, 1)], 0.0, ALU.is_equal, ALU.add,
                                accum_out=count[:, ds(k, 1)]).then_inc(s_count, 1)
            dve.wait_ge(s_prefix, 1)
            v.tensor_copy(total_i, psum[:, 0, 0:NK]).then_inc(s_v, 1)
            dve.wait_ge(s_v, 4)
            v.tensor_scalar(total_i, total_i, SUPER - 1, None, ALU.add).then_inc(s_v, 1)
            dve.wait_ge(s_v, 5)
            v.tensor_scalar(total_i, total_i, SHIFT, None, ALU.arith_shift_right).then_inc(s_v, 1)
            dve.wait_ge(s_v, 6)
            v.tensor_copy(groups_f, total_i).then_inc(s_v, 1)
            dve.wait_ge(s_v, 7)
            v.tensor_tensor_scan(first_group, ones_mat[:, 0:NK], groups_f, 0.0, ALU.mult, ALU.add).then_inc(s_v, 1)
            dve.wait_ge(s_v, 8)
            v.tensor_tensor(first_group, first_group, groups_f, ALU.subtract).then_inc(s_start, 1)
            dve.wait_ge(s_start, 1)
            v.tensor_scalar(before, psum[:, 0, NK:2 * NK], -1.0, None, ALU.add).then_inc(s_v, 1)
            dve.wait_ge(s_v, 9)
            v.scalar_tensor_tensor(out=before, in0=first_group, scalar=float(SUPER), in1=before,
                                   op0=ALU.mult, op1=ALU.add).then_inc(s_v, 1)
            dve.wait_ge(s_startT, 1)
            v.tensor_copy(first_col[0:NK, :], psum[0:NK, 1, 0:1]).then_inc(s_v, 1)
            dve.wait_ge(s_v, 11)
            v.tensor_scalar(started[0:NK, :], group_no[0:NK, :], first_col[0:NK, 0:1], None, ALU.is_ge).then_inc(s_began, 1)
            dve.wait_ge(s_gb, 1)
            v.tensor_scalar(group_bucket[:, :], psum[:, 2, 0:GROUPS], -1.0, None, ALU.add).then_inc(s_v, 1)
            for c, (step0, steps) in enumerate(chunks):
                width = steps * STEP
                cols = slice(step0 * STEP, step0 * STEP + width)
                with dve.Fori(0, NK // 2) as k:
                    n = k * 8 + c * 4 * NK + 1
                    dve.wait_ge(s_scan, n)
                    for h in range(2):
                        v.tensor_scalar(same[h][:, 0:width], block_b[:, cols], bucket_no[:, ds(k * 2 + h, 1)], None, ALU.is_equal).then_inc(s_scan, 1)
                    for h in range(2):
                        dve.wait_ge(s_scan, n + 1 + h)
                        v.tensor_tensor_scan(scan[h][:, 0:width], ones_row[:, 0:width], same[h][:, 0:width], before[:, ds(k * 2 + h, 1)], ALU.mult, ALU.add).then_inc(s_scan, 1)
                    for h in range(2):
                        dve.wait_ge(s_scan, n + 3 + 3 * h)
                        dve.sem_inc(s_passed, 1)
                        v.tensor_copy(before[:, ds(k * 2 + h, 1)], scan[h][:, width - 1:width]).then_inc(s_scan, 1)
                        v.copy_predicated(slot[:, cols], same[h][:, 0:width], scan[h][:, 0:width]).then_inc(s_scan, 1)
                dve.wait_ge(s_scan, (c + 1) * 4 * NK + 1)
                v.engine_nop().then_inc(s_slots, steps)
            v.memset(sums[:, :, :], 0.0).then_inc(s_sums0, 1)
            dve.wait_ge(s_sums0, 1)
            v.engine_nop().then_inc(s_free, RING)

            def features(i, r):
                dve.wait_ge(s_xg[r], i * 16 * LANE + 16 * LANE)
                s_part = xx[r][:, :, 0:S]
                v_part = xx[r][:, :, S:D].rearrange("p j (u i) -> p j u i", i=3)
                v.tensor_tensor(vprod[r].rearrange("p j (u i) -> p j u i", i=3), v_part,
                                spread(rec[r][:, :, 0:3], 2, V), ALU.mult).then_inc(s_vp, 1)
                v.tensor_tensor(xr[r][:, :, 0:3 * S].rearrange("p j (i u) -> p j i u", u=S), spread(s_part, 2, 3),
                                spread(rec[r][:, :, 0:3], 3, S), ALU.mult)
                v.tensor_tensor(hot[r], spread(iota[:, :], 1, LANE), spread(rec[r][:, :, 5], 2, P), ALU.is_equal)
                dve.wait_ge(s_vp, i * RING + r + 1)
                v.tensor_reduce(xr[r][:, :, 3 * S:3 * S + V], vprod[r].rearrange("p j (u i) -> p j u i", i=3), AX_X,
                                ALU.add).then_inc(s_xr, 1)

            def add_group(q, r):
                bucket = dve.value_load(group_bucket[0:1, ds(q, 1)], min_val=0, max_val=NK - 1)
                dve.wait_ge(s_grp, q + 1)
                dve.wait_ge(s_free, q + RING)
                to = sums[:, ds(bucket, 1), :].rearrange("p o c -> p (o c)")
                bank = 2 * (r % 2)
                v.tensor_tensor(to[:, 0:SUMS_A], to[:, 0:SUMS_A], psum[:, bank, 0:SUMS_A], ALU.add)
                v.tensor_tensor(to[:, SUMS_A:SUMS], to[:, SUMS_A:SUMS], psum[:, bank + 1, 0:SUMS - SUMS_A], ALU.add).then_inc(s_free, 1)

            for r in range(RING):
                features(0, r)
                if r:
                    add_group(r - 1, r - 1)
            with dve.Fori(1, GROUPS // RING) as i:
                for r in range(RING):
                    features(i, r)
                    add_group(i * RING + r - 1, (r - 1) % RING)
            add_group(GROUPS - 1, RING - 1)

            dve.wait_ge(s_free, GROUPS + RING)
            for t in w_msg + w_lin:
                last = v.memset(t, 0.0)
            last.then_inc(s_w, 1)
            v.engine_nop().then_inc(s_zfree, ZRING)
            dve.wait_ge(s_wready, 1)

            def finish(b, p):
                dve.wait_ge(s_u, b + 1)
                v.tensor_tensor(y2, psum[:, 7, 0:D], rr[p], ALU.add).then_inc(s_y, 1)
                yield
                dve.wait_ge(s_y, b * 5 + 1)
                v.tensor_tensor(y1[p][:, 0:S], y1[p][:, 0:S], y2[:, 0:S], ALU.add)
                y1v = y1[p][:, S:D].rearrange("p (w i) -> p i w", i=3)
                v.tensor_tensor(y1v, y1v, y2[:, S:D].rearrange("p (i w) -> p i w", i=3), ALU.add).then_inc(s_y, 1)
                yield
                dve.wait_ge(s_y, b * 5 + 2)
                v.bn_stats(stats, y1[p]).then_inc(s_y, 1)
                yield
                dve.wait_ge(s_y, b * 5 + 3)
                dve.sem_inc(s_passed, 1)
                v.bn_aggr(moments, stats).then_inc(s_y, 1)
                yield
                dve.wait_ge(s_y, b * 5 + 4)
                v.tensor_scalar(moments[:, 1:2], moments[:, 1:2], EPS, None, ALU.add).then_inc(s_var, 1)
                yield
                dve.wait_ge(s_std, b + 1)
                v.reciprocal(rstd, std).then_inc(s_y, 1)
                yield
                dve.wait_ge(s_y, b * 5 + 5)
                v.tensor_scalar(xall[:, ds(b, 1), :].rearrange("p o c -> p (o c)"), y1[p], moments[:, 0:1], rstd, ALU.subtract,
                                ALU.mult).then_inc(s_done, 1)

            def update(b, p, ending):
                a0 = agg[p][:, 0:S]
                a1 = agg[p][:, S:D].rearrange("p (i v) -> p i v", i=3)
                xv = blk_x[p][:, S:D].rearrange("p (u i) -> p i u", i=3)
                pu = prod_u.rearrange("p (i w k) -> p i w k", i=3, k=2 * V)
                rr0, rr1 = rr[p][:, 0:S], rr[p][:, S:D].rearrange("p (i w) -> p i w", w=V)
                W0, W1 = BANK // S, BANK // V
                dve.wait_ge(s_agc, b + 1)
                dve.wait_ge(s_main, b + 1)

                def reduce_ss(z):
                    dve.wait_ge(s_zfree, b * ZALL + ZRING + z + 1)
                    w = z // 2 * W0 + z % 2 * V
                    v.tensor_reduce(rr0[:, w:w + W0], prod_ss[z % 2].rearrange("p (w k) -> p w k", k=S), AX_X,
                                    ALU.add).then_inc(s_red, 1)

                for z in range(ZSS):
                    if z >= 2:
                        dve.wait_ge(s_red, b * RED + z - 1)
                    dve.wait_ge(s_z, b * ZALL + z + 1)
                    v.tensor_tensor(prod_ss[z % 2].rearrange("p (w k) -> p w k", k=S),
                                    psum[:, z % ZRING, :].rearrange("p (w k) -> p w k", k=S), spread(a0, 1, W0),
                                    ALU.mult).then_inc(s_zfree, 1)
                    if z:
                        reduce_ss(z - 1)
                        next(ending, None)
                for c in range(ZU):
                    for k, other in enumerate((a1, xv)):
                        z = ZSS + 2 * c + k
                        if k == 0 and c:
                            dve.wait_ge(s_red, b * RED + ZSS + c)
                        dve.wait_ge(s_z, b * ZALL + z + 1)
                        for m in range(3):
                            last = v.tensor_tensor(pu[:, m, :, k * V:(k + 1) * V],
                                                   psum[:, z % ZRING, :].rearrange("p (w k) -> p w k", k=V),
                                                   spread(other[:, m], 1, W1), ALU.mult)
                        last.then_inc(s_zfree, 1)
                        if z == ZSS:
                            reduce_ss(ZSS - 1)
                        if c and k:
                            v.tensor_scalar(y1[p], blk_x[p], 2.0, None, ALU.mult)
                    dve.wait_ge(s_zfree, b * ZALL + ZRING + z + 1)
                    v.tensor_reduce(rr1[:, :, c * W1:(c + 1) * W1], pu, AX_X, ALU.add).then_inc(s_red if c < ZU - 1 else s_main, 1)

            update(0, 0, iter(()))
            update(1, 1, finish(0, 0))
            with dve.Fori(1, NU // 2) as i:
                update(i * 2, 0, finish(i * 2 - 1, 1))
                update(i * 2 + 1, 1, finish(i * 2, 0))
            dve.wait_ge(s_main, NU + 1)
            for _ in finish(NU - 1, 1):
                pass

        @block.tensor
        def _(pe):
            t = nc.tensor
            pe.wait_ge(s_const, CONSTS)
            pe.wait_ge(s_count, NK + 1)
            t.matmul(psum[:, 0, 0:NK], ones_mat, count, start=True, stop=True)
            t.matmul(psum[:, 0, NK:2 * NK], lower, count, start=True, stop=True).then_inc(s_prefix, 1)
            pe.wait_ge(s_start, 1)
            t.transpose(psum[0:NK, 1, 0:P], first_group, ident[:, :]).then_inc(s_startT, 1)
            pe.wait_ge(s_began, 1)
            t.matmul(psum[:, 2, 0:GROUPS], ones_mat[0:NK, :], started[0:NK, :], start=True, stop=True).then_inc(s_gb, 1)

            with pe.Fori(0, GROUPS // RING) as i:
                for r in range(RING):
                    q = i * RING + r
                    bank = 2 * (r % 2)
                    pe.wait_ge(s_xr, q + 1)
                    pe.wait_ge(s_xd, q + 1)
                    pe.wait_ge(s_free, q + RING - 1)
                    for j in range(LANE):
                        first, end = j == 0, j == LANE - 1
                        t.matmul(psum[:, bank, 0:SUMS_A], hot[r][:, j, :], xx[r][:, j, :], start=first, stop=end, skip_group_check=True)
                        last = t.matmul(psum[:, bank + 1, 0:SUMS - SUMS_A], hot[r][:, j, :], xr[r][:, j, :], start=first, stop=end,
                                        skip_group_check=True)
                    last.then_inc(s_grp, 1)

            pe.wait_ge(s_wready, 1)
            turned = [(P, 2 * D, 3 * P), (S, 0, 0), (S, D, P), (3 * V, S, 4 * P), (3 * V, D + S, 5 * P),
                      (3 * V, 2 * D + 2 * S, 6 * P)]
            weight_of = [4, 0, 2, 1, 3, 5]

            def turn(b, p):
                pe.wait_ge(s_blk, b + 1)
                for rows, c, to in turned:
                    t.transpose(psum[0:rows, 4 + to // BANK, to % BANK:to % BANK + P], blk_sum[:, c:c + rows], ident[:, :])
                t.transpose(psum[0:S, 4, 2 * P:3 * P], blk_x[p][:, 0:S], ident[:, :])
                t.transpose(psum[0:3 * V, 5, 3 * P:4 * P], blk_x[p][:, S:D], ident[:, :]).then_inc(s_t, 1)

            def messages(b, p):
                pe.wait_ge(s_tt, b + 1)
                for n, (rows, c, to) in enumerate(turned):
                    last = t.matmul(psum[:, 6, 0:D], flip[p][0:rows, to:to + P], w_msg[weight_of[n]][0:rows, :],
                                    start=(n == 0), stop=(n == len(turned) - 1))
                last.then_inc(s_ag, 1)

            def turn_a0(b, p):
                pe.wait_ge(s_const, CONSTS)
                pe.wait_ge(s_agc, b + 1)
                t.transpose(psum[0:S, 6, 256:256 + P], agg[p][:, 0:S], ident[:, :]).then_inc(s_a0, 1)

            def products(b, p, z0, z1):
                for z in range(z0, z1):
                    pe.wait_ge(s_zfree, b * ZALL + z + 1)
                    if z < ZSS:
                        half = slice(z % 2 * S, z % 2 * S + S)
                        lhs, rhs = flip[p][half, 2 * P:3 * P], w_ss[half, z // 2 * BANK:(z // 2 + 1) * BANK]
                    else:
                        c, k = (z - ZSS) // 2, (z - ZSS) % 2
                        rhs = w_u1[k * S:k * S + S, c * BANK:(c + 1) * BANK]
                        lhs = a0_t[p][S:P, :] if k else flip[p][0:S, 2 * P:3 * P]
                    t.matmul(psum[:, z % ZRING, :], lhs, rhs, start=True, stop=True).then_inc(s_z, 1)

            turn(0, 0)
            messages(0, 0)
            turn_a0(0, 0)
            with pe.Fori(0, NU // 2) as i:
                for p in range(2):
                    b = i * 2 + p
                    products(b, p, 0, 3)
                    pe.wait_ge(s_gtc, b * 2 + 1)
                    turn(b + 1, 1 - p)
                    products(b, p, 3, 5)
                    pe.wait_ge(s_a0c, b + 1)
                    messages(b + 1, 1 - p)
                    products(b, p, 5, 7)
                    turn_a0(b + 1, 1 - p)
                    products(b, p, 7, 9)
                    pe.wait_ge(s_g, b * 5 + 5)
                    for c in range(8):
                        last = t.transpose(psum[:, 4 + c // 4, c % 4 * P:c % 4 * P + P], gram[:, c * P:(c + 1) * P], ident[:, :])
                        if c % 4 == 3:
                            last.then_inc(s_gt, 1)
                    products(b, p, 9, 11)
                    pe.wait_ge(s_done, b + 1)
                    t.matmul(psum[:, 7, 0:D], flip[p][0:S, 2 * P:3 * P], w_lin[0][0:S, :], start=True, stop=False, skip_group_check=True)
                    t.matmul(psum[:, 7, 0:D], flip[p][0:3 * V, 7 * P:8 * P], w_lin[1][0:3 * V, :], start=False, stop=False,
                             skip_group_check=True)
                    for c in range(8):
                        if c % 4 == 0:
                            pe.wait_ge(s_gtc, b * 2 + c // 4 + 2)
                        last = t.matmul(psum[:, 7, 0:S], gram_t[c // 4][:, c % 4 * P:c % 4 * P + P], w_vv[:, c, :],
                                        start=False, stop=(c == 7), skip_group_check=True)
                    last.then_inc(s_u, 1)
                    products(b, p, 11, ZALL)


_INS = ['x', 'src', 'dst', 'edge_attr_4', 'node_vec1', 'L0_gnn_Wm_ss', 'L0_gnn_Wm_vv', 'L0_gnn_Wm_sv', 'L0_gnn_Wm_vs',
        'L0_gnn_Lm_s', 'L0_gnn_Lm_v', 'L0_gnn_Wu_ss', 'L0_gnn_Wu_vv', 'L0_gnn_Wu_sv', 'L0_gnn_Wu_vs', 'L0_gnn_Lu_s',
        'L0_gnn_Lu_v']


def kernel(**inputs):
    import numpy as _np
    import concourse.bacc as _bacc
    from concourse import mybir as _mybir
    from concourse.bass_utils import run_bass_kernel_spmd as _run

    nc = _bacc.Bacc("TRN2", target_bir_lowering=False, num_devices=1)
    arrays, args = {}, []
    for name in _INS:
        a = _np.ascontiguousarray(inputs[name])
        arrays[f"in_{name}_dram"] = a
        args.append(nc.dram_tensor(f"in_{name}_dram", a.shape, _mybir.dt.from_np(a.dtype), kind="ExternalInput").ap())
    out = nc.dram_tensor("out_0_dram", inputs['x'].shape, _mybir.dt.float32, kind="ExternalOutput").ap()
    gnn_kernel(nc, *args, out)
    r = _run(nc, [arrays], core_ids=[0])
    return r.results[0]["out_0_dram"]
```

```python
from contextlib import ExitStack

import concourse.bass as bass
from concourse import mybir

P = 128
LANE = 4
SUPER = P * LANE
SHIFT = SUPER.bit_length() - 1
BITS = P.bit_length() - 1
STEP = 13
FIRST_STEPS = (4, 12)
CHUNK_STEPS = 27
REC = 6
RING = 4
S, V = 64, 32
D = S + 3 * V
SR, VR = 2 * D, 2 * D + 3 * S
SUMS = VR + V
SUMS_A = 2 * D
BANK = 512
ZSS, ZU = S * S // BANK, V * V // BANK
ZALL = ZSS + 2 * ZU
ORDER = [("s", n) for n in range(ZSS // 2)] + [("u", 0, 0), ("u", 0, 1)] + \
        [("s", n) for n in range(ZSS // 2, ZSS)] + [("u", 1, 0), ("u", 1, 1)]
ZRING = 4
PAIRS = ZSS // 2
REGION = 17048
EPS = 1e-5
INV_SQRT3, INV8, INV_SQRT32 = 0.5773502691896258, 0.125, 0.17677669529663687
INV64, INV32, INV_SQRT2048 = 0.015625, 0.03125, 0.022097086912079608

ALU = mybir.AluOpType
ACT = mybir.ActivationFunctionType
F32, BF16 = mybir.dt.float32, mybir.dt.bfloat16
I32, U32, U16 = mybir.dt.int32, mybir.dt.uint32, mybir.dt.uint16
AX_X = mybir.AxisListType.X
ds = bass.ds


def spread(ap, axis, n):
    ap = ap.unsqueeze(axis)
    shape = list(ap.shape)
    shape[axis] = n
    return ap.to_broadcast(shape)


def gnn_kernel(nc, x, src, dst, attr, node_vec, Wm_ss, Wm_vv, Wm_sv, Wm_vs, Lm_s, Lm_v,
               Wu_ss, Wu_vv, Wu_sv, Wu_vs, Lu_s, Lu_v, out):
    N, E = x.shape[0], src.shape[0]
    NB = -(-N // P)
    NK = NB + 1 + (NB + 1) % 2
    NU = NB + NB % 2
    NX = NU + 1
    NTAIL = N - (NB - 1) * P
    STEPS = -(-(-(-E // P)) // STEP)
    STEPS += STEPS % 2
    COLS = STEPS * STEP
    CHUNK = CHUNK_STEPS * STEP
    chunks = []
    while not chunks or sum(chunks[-1]) < STEPS:
        at = sum(chunks[-1]) if chunks else 0
        n = FIRST_STEPS[len(chunks)] if len(chunks) < len(FIRST_STEPS) else CHUNK_STEPS
        chunks.append((at, min(n, STEPS - at)))
    FULL = E // COLS
    REST = E - FULL * COLS
    assert FULL == P - 1 and 0 < REST < COLS and NX <= NK + 1
    GROUPS = -(-(P * COLS // SUPER + NK) // RING) * RING
    assert GROUPS <= BANK
    SLOTS = GROUPS * SUPER

    table = nc.dram_tensor("edge_table", (SLOTS, REC), F32, kind="Internal").ap()
    groups_of_table = table.rearrange("(q p j) w -> q p (j w)", p=P, j=LANE)

    ctx = ExitStack()
    with ctx:
        def sb(name, shape, dt=F32):
            return ctx.enter_context(nc.sbuf_tensor(name, shape, dt))

        def sem(name):
            return ctx.enter_context(nc.semaphore(name))

        xall = sb("xall", [P, NX, D])
        sums = sb("sums", [P, NK + 1, SUMS])
        ident = sb("ident", [P, P])
        iota = sb("iota", [P, P])
        region = sb("region", [P, REGION])

        place = [0]

        def carve(shape, dt=F32):
            n = 1
            for d in shape:
                n *= d
            words = n if dt in (F32, I32, U32) else -(-n // 2)
            v = region[:, place[0]:place[0] + words]
            place[0] += -(-words // 8) * 8
            assert place[0] <= REGION, place[0]
            if dt is not F32:
                v = v.bitcast(dt)[:, 0:n]
            if len(shape) == 2:
                v = v.rearrange("p (a b) -> p a b", b=shape[1])
            if len(shape) == 3:
                v = v.rearrange("p (a b c) -> p a b c", b=shape[1], c=shape[2])
            return v

        group_bucket = region[:, REGION - GROUPS:REGION].bitcast(I32)

        row_i = carve([COLS], I32)
        col_i = carve([COLS], I32)
        attr_s = carve([COLS, 4])
        block_b = carve([COLS], BF16)
        slot = carve([COLS])
        ones_row = carve([CHUNK])
        same = [carve([CHUNK], U16) for _ in range(2)]
        scan = [carve([CHUNK]) for _ in range(2)]
        junk = slot.bitcast(BF16)[:, 0:COLS]
        FILL = GROUPS // 4 * LANE // 4
        empty = carve([FILL, REC])
        bucket_no = carve([NK])
        count = carve([NK])
        total_i = carve([NK], I32)
        groups_f = carve([NK])
        first_group = carve([NK])
        before = carve([NK])
        ones_mat = carve([P])
        lower = carve([P])
        first_col = carve([1])
        group_no = carve([GROUPS])
        started = carve([GROUPS])
        stage_rec = [carve([STEP, REC]) for _ in range(2)]
        stage_slot = [carve([STEP], I32) for _ in range(2)]

        assert place[0] <= REGION - GROUPS, place[0]

        place[0] = 0
        rec = [carve([LANE, REC]) for _ in range(RING)]
        xx = [carve([LANE, 2 * D]) for _ in range(RING)]
        xr = [carve([LANE, 3 * S + V]) for _ in range(RING)]
        hot = [carve([LANE, P]) for _ in range(RING)]
        vprod = [carve([LANE, 3 * V]) for _ in range(RING)]

        assert place[0] <= REGION - GROUPS, place[0]

        place[0] = 0
        w_ss = carve([S * S // 2])
        w_u1 = carve([V * V])
        w_vv = carve([V * V // P, S])
        w_msg = [carve([D]) for _ in range(6)]
        w_lin = [carve([D]) for _ in range(2)]
        blk_sum = carve([SUMS])
        blk_x = [carve([D]) for _ in range(2)]
        flip = carve([6 * P])
        xs_low = [carve([P]) for _ in range(2)]
        xs_high = [carve([P]) for _ in range(2)]
        xv_t = [carve([P]) for _ in range(2)]
        agg = [carve([D]) for _ in range(2)]
        a0_t = [carve([P]) for _ in range(2)]
        gram = carve([V * V])
        gram_t = [carve([BANK]) for _ in range(2)]
        gtmp = carve([V * V])
        rr = [carve([D]) for _ in range(2)]
        y1 = [carve([D]) for _ in range(2)]
        y2 = carve([D])
        stats = carve([6])
        moments = carve([2])
        std = carve([1])
        rstd = carve([1])
        at = place[0]
        prod_ss = [carve([BANK]) for _ in range(4)]
        prod_u = carve([3 * (BANK // V) * 2 * V])
        place[0] = at
        raw_u1 = carve([V * V])

        psum = ctx.enter_context(nc.psum_tensor("psum", [P, 8, BANK], F32))

        s_passed = sem("wait_passed")
        s_pad = sem("edge_pads_cleared")
        s_edges = sem("edges_loaded")
        s_attr = sem("attributes_loaded")
        s_x = sem("x_loaded")
        s_const = sem("constants_ready")
        s_empty = sem("empty_records_ready")
        s_table = sem("table_cleared")
        s_v = sem("vector_chain")
        s_count = sem("edges_counted")
        s_prefix = sem("prefixes_ready")
        s_start = sem("group_starts_ready")
        s_startT = sem("group_starts_turned")
        s_began = sem("started_ready")
        s_gb = sem("group_buckets_summed")
        s_slots = sem("slots_ready")
        s_scan = sem("scan_chain")
        s_staged = sem("records_staged")
        s_scattered = [sem(f"records_scattered{h}") for h in range(2)]
        s_sums0 = sem("sums_cleared")
        s_rec = [sem(f"records_loaded{r}") for r in range(RING)]
        s_xg = [sem(f"x_gathered{r}") for r in range(RING)]
        s_xd = sem("x_times_dist_ready")
        s_vp = sem("v_products_ready")
        s_xr = sem("edge_features_ready")
        s_grp = sem("group_summed")
        s_free = sem("group_buffers_free")
        s_w = sem("weights_cleared")
        s_wload = sem("weights_loaded")
        s_wready = sem("weights_ready")
        s_blk = sem("block_staged")
        s_t = sem("block_turned")
        s_tt = sem("turned_block_copied")
        s_ag = sem("messages_summed")
        s_agc = sem("messages_copied")
        s_a0 = sem("a0_turned")
        s_a0c = sem("a0_turned_copied")
        s_z = sem("product_bank_ready")
        s_zfree = sem("product_banks_free")
        s_pair = sem("product_pairs_added")
        s_psum = sem("product_pairs_summed")
        s_red = sem("products_reduced")
        s_g = sem("gram_chain")
        s_gt = sem("gram_turned")
        s_gtc = sem("gram_turned_copied")
        s_u = sem("update_summed")
        s_main = sem("block_products_done")
        s_y = sem("norm_chain")
        s_var = sem("variance_ready")
        s_std = sem("deviation_ready")
        s_done = sem("block_done")
        s_store = sem("stored")

        CONSTS = 8

        block = ctx.enter_context(nc.Block())

        def weight_loads():
            for h in range(2):
                yield (w_ss[h * S:h * S + S, :].rearrange("p (z k) -> p z k", k=BANK),
                       Wu_ss.rearrange("u v w -> u (v w)").rearrange("u (z h k) -> u z h k", h=2, k=BANK)[:, :, h, :])
            yield raw_u1[0:S, :], Wu_sv.rearrange("u v w -> u (v w)")
            yield raw_u1[S:P, :].rearrange("p (u w) -> p u w", w=V), Wu_vs.rearrange("u v w -> v u w")
            yield w_vv, Wu_vv.rearrange("u v w -> (u v) w").rearrange("(c p) w -> p c w", p=P)
            yield w_msg[0][0:S, 0:S], Lm_s
            yield w_msg[2][0:S, 0:S], Wm_ss
            for i in range(2):
                yield w_msg[4][S * i:S * i + S, S + V * i:S + V * i + V], Wm_sv
            yield w_msg[5][0:S, S + 2 * V:D], Wm_sv
            yield w_msg[5][S:S + V, 0:S], Wm_vv
            yield w_lin[0][0:S, 0:S], Lu_s
            for i in range(3):
                c = slice(S + V * i, S + V * i + V)
                yield w_msg[1][i:3 * V:3, c], Lm_v
                yield w_msg[3][i:3 * V:3, c], Wm_vs
                yield w_lin[1][i:3 * V:3, c], Lu_v

        WLOADS = len(list(weight_loads()))

        @block.sync
        def _(sp):
            for s in (s_count, s_scan, s_gt, s_gtc, s_main, s_done):
                sp.sem_inc(s, 1)
            sp.wait_ge(s_pad, 1)
            for tile_, dram in ((row_i, src), (col_i, dst)):
                sp.dma_start(tile_[0:FULL, :], dram[0:FULL * COLS].rearrange("(p t) -> p t", t=COLS)).then_inc(s_edges, 16)
                sp.dma_start(tile_[FULL:P, 0:REST], dram[FULL * COLS:E].rearrange("(p t) -> p t", p=1)).then_inc(s_edges, 16)
            sp.dma_start(attr_s[0:FULL, :, :], attr[0:FULL * COLS, :].rearrange("(p t) w -> p t w", t=COLS)).then_inc(s_attr, 16)
            sp.dma_start(attr_s[FULL:P, 0:REST, :], attr[FULL * COLS:E, :].rearrange("(p t) w -> p t w", p=1)).then_inc(s_attr, 16)
            sp.wait_ge(s_empty, 3)
            rows = SLOTS // P
            flat = table.rearrange("(p r) w -> p r w", r=rows)
            for c in range(rows // FILL):
                sp.dma_start(flat[:, c * FILL:(c + 1) * FILL, :], empty).then_inc(s_table, 16)
            sp.wait_ge(s_const, CONSTS)
            sp.dma_start(xall[:, 0:NB - 1, :], x[0:(NB - 1) * P, :].rearrange("(b p) d -> p b d", p=P)).then_inc(s_x, 16)
            sp.dma_start(xall[0:NTAIL, NB - 1, :], x[(NB - 1) * P:N, :]).then_inc(s_x, 16)

            for h in range(2):
                sp.wait_ge(s_scattered[h], 16 * STEP * (STEPS // 2))
            with sp.Fori(0, GROUPS // RING) as i:
                for r in range(RING):
                    sp.wait_ge(s_free, i * RING + r + 1)
                    sp.dma_start(rec[r].rearrange("p j w -> p (j w)"),
                                 groups_of_table[ds(i * RING + r, 1)].rearrange("q p f -> (q p) f")).then_inc(s_rec[r], 16)

            sp.wait_ge(s_w, 1)
            with nc.allow_non_contiguous_dma(reason="small weights"):
                for to, frm in weight_loads():
                    sp.dma_start(to, frm).then_inc(s_wload, 16)
            pairs = NU // 2
            with sp.Fori(0, pairs - 1) as i:
                sp.wait_ge(s_done, 2 * i + 3)
                sp.dma_start(out[ds(i * 2 * P, 2 * P), :].rearrange("(b p) d -> p b d", p=P),
                             xall[:, ds(i * 2, 2), :]).then_inc(s_store, 16)
            sp.wait_ge(s_done, NU + 1)
            stores = pairs - 1
            for b in range(NU - 2, NB):
                n = min(P, N - b * P)
                sp.dma_start(out[b * P:b * P + n, :], xall[0:n, b, :]).then_inc(s_store, 16)
                stores += 1
            sp.wait_ge(s_store, 16 * stores)

        @block.gpsimd
        def _(pool):
            g = nc.gpsimd
            g.iota(iota[:, :], [[1, P]], base=0, channel_multiplier=0, allow_small_or_imprecise_dtypes=True).then_inc(s_const, 1)
            g.iota(bucket_no, [[1, NK]], base=0, channel_multiplier=0, allow_small_or_imprecise_dtypes=True).then_inc(s_const, 1)
            g.iota(group_no, [[1, GROUPS]], base=0, channel_multiplier=0, allow_small_or_imprecise_dtypes=True).then_inc(s_const, 1)
            g.memset(ones_mat, 1.0).then_inc(s_const, 1)
            g.memset(ones_row, 1.0).then_inc(s_const, 1)
            pool.wait_ge(s_const, 5)
            g.affine_select(out=lower, in_=ones_mat, pattern=[[1, P]], compare_op=ALU.is_gt, fill=0.0,
                            base=0, channel_multiplier=-1).then_inc(s_const, 1)
            g.affine_select(out=ident[:, :], in_=ones_mat, pattern=[[1, P]], compare_op=ALU.is_equal, fill=0.0,
                            base=0, channel_multiplier=-1).then_inc(s_const, 1)
            g.memset(xall[:, NB - 1:NX, :], 0.0).then_inc(s_const, 1)
            pool.wait_ge(s_table, 16 * (SLOTS // P // FILL))
            with pool.Fori(0, STEPS // 2) as i:
                for h in range(2):
                    pool.wait_ge(s_staged, i * 2 + h + 1)
                    pool.sem_inc(s_passed, 1)
                    for j in range(STEP):
                        g.indirect_dma_start(
                            out=table, out_offset=bass.IndirectOffsetOnAxis(ap=stage_slot[h][:, j:j + 1].bitcast(U32), axis=0),
                            in_=stage_rec[h][:, j, :], in_offset=None).then_inc(s_scattered[h], 16)
            with pool.Fori(0, GROUPS // RING) as i:
                for r in range(RING):
                    pool.wait_ge(s_rec[r], i * 16 + 16)
                    pool.sem_inc(s_passed, 1)
                    for j in range(LANE):
                        g.indirect_dma_start(
                            out=xx[r][:, j, 0:D], out_offset=None, in_=x,
                            in_offset=bass.IndirectOffsetOnAxis(ap=rec[r][:, j, 4:5].bitcast(U32), axis=0)).then_inc(s_xg[r], 16)
            with pool.Fori(0, NU // 2) as i:
                for p in range(2):
                    xv = blk_x[p][:, S:D].rearrange("p (u i) -> p u i", i=3)
                    a1 = agg[p][:, S:D].rearrange("p (i v) -> p i v", i=3)
                    def add_pair(k):
                        pool.wait_ge(s_zfree, i * 2 * ZALL + p * ZALL + ZRING + ORDER.index(("s", 2 * k + 1)) + 1)
                        a, c = prod_ss[2 * k % 4], prod_ss[2 * k % 4 + 1]
                        g.tensor_tensor(a, a, c, ALU.add).then_inc(s_pair, 1)

                    gm, gt = gram.rearrange("p (u v) -> p u v", v=V), gtmp.rearrange("p (u v) -> p u v", v=V)
                    add_pair(0)
                    add_pair(1)
                    n = i * 10 + p * 5
                    pool.wait_ge(s_agc, i * 2 + p + 1)
                    pool.wait_ge(s_gt, i * 4 + 2 * p + 1)
                    for c in range(3):
                        if c == 2:
                            add_pair(2)
                            add_pair(3)
                        to = gt if c else gm
                        if c == 2:
                            pool.wait_ge(s_g, n + 3)
                        g.tensor_tensor(to, spread(xv[:, :, c], 2, V), spread(a1[:, c, :], 1, V), ALU.mult).then_inc(s_g, 1)
                        if c:
                            pool.wait_ge(s_g, n + 2 * c)
                            g.tensor_tensor(gm, gm, gt, ALU.add).then_inc(s_g, 1)

        @block.scalar
        def _(act):
            a = nc.scalar
            act.wait_ge(s_attr, 32)
            act.wait_ge(s_edges, 64)
            def stage(i):
                for h in range(2):
                    cols = ds(i * 2 * STEP + h * STEP, STEP)
                    act.wait_ge(s_slots, i * 2 + h + 1)
                    if type(i) is not int:
                        act.wait_ge(s_scattered[h], i * 16 * STEP)
                    a.activation(stage_rec[h][:, :, 0:4], attr_s[:, cols, :], ACT.Copy)
                    a.activation(stage_rec[h][:, :, 4].bitcast(I32), col_i[:, cols], ACT.Copy)
                    a.activation(stage_rec[h][:, :, 5], row_i[:, cols], ACT.Copy)
                    a.activation(stage_slot[h], slot[:, cols], ACT.Copy).then_inc(s_staged, 1)

            stage(0)
            with act.Fori(1, STEPS // 2) as i:
                stage(i)
            with act.Fori(0, GROUPS // RING) as i:
                for r in range(RING):
                    act.wait_ge(s_xg[r], i * 16 * LANE + 16 * LANE)
                    for j in range(LANE):
                        last = a.activation(xx[r][:, j, D:2 * D], xx[r][:, j, 0:D], ACT.Copy, scale=rec[r][:, j, 3:4])
                    last.then_inc(s_xd, 1)

            act.wait_ge(s_wload, 16 * WLOADS)
            a.activation(w_ss, w_ss, ACT.Copy, scale=INV64)
            a.activation(w_u1.rearrange("p (w v) -> p w v", v=V), raw_u1.rearrange("p (v w) -> p w v", w=V), ACT.Copy,
                         scale=INV_SQRT2048)
            a.activation(w_vv, w_vv, ACT.Copy, scale=INV_SQRT3 * INV32)
            for k, rows, factor in ((0, slice(0, S), INV8), (1, slice(0, 3 * V), INV_SQRT32), (2, slice(0, S), INV8),
                                    (3, slice(0, 3 * V), INV_SQRT32), (4, slice(0, P), INV8), (5, slice(0, S), INV8),
                                    (5, slice(S, S + V), INV_SQRT3 * INV_SQRT32)):
                a.activation(w_msg[k][rows, :], w_msg[k][rows, :], ACT.Copy, scale=factor)
            a.activation(w_lin[0][0:S, :], w_lin[0][0:S, :], ACT.Copy, scale=INV8)
            a.activation(w_lin[1][0:3 * V, :], w_lin[1][0:3 * V, :], ACT.Copy, scale=INV_SQRT32).then_inc(s_wready, 1)
            act.wait_ge(s_x, 32)

            for h in range(2):
                for z in (xs_low[h][S:P, :], xs_high[h][0:S, :], a0_t[h][0:S, :]):
                    a.activation(z, ident[0:S, :], ACT.Copy, scale=0.0)

            def ahead(b, p, after=lambda: None):
                if not (type(b) is int and b == 0):
                    act.wait_ge(s_t, b)
                a.activation(blk_sum, sums[:, ds(b, 1), :].rearrange("p o c -> p (o c)"), ACT.Copy)
                if not (type(b) is int and b == 0):
                    act.wait_ge(s_main, b)
                a.activation(blk_x[p], xall[:, ds(b, 1), :].rearrange("p o c -> p (o c)"), ACT.Copy).then_inc(s_blk, 1)
                act.wait_ge(s_t, b + 1)
                a.activation(xs_low[p][0:S, :], psum[0:S, 5, 3 * P:BANK], ACT.Copy)
                a.activation(xs_high[p][S:P, :], psum[0:S, 5, 3 * P:BANK], ACT.Copy)
                a.activation(flip[:, 0:P], psum[:, 5, 2 * P:3 * P], ACT.Copy)
                a.activation(flip[0:S, P:3 * P], psum[0:S, 5, 0:2 * P], ACT.Copy)
                a.activation(flip[0:3 * V, 3 * P:6 * P], psum[0:3 * V, 4, 0:3 * P], ACT.Copy)
                a.activation(xv_t[p][0:3 * V, :], psum[0:3 * V, 4, 3 * P:BANK], ACT.Copy).then_inc(s_tt, 1)
                act.wait_ge(s_ag, b + 1)
                a.activation(agg[p], psum[:, 6, 0:D], ACT.Copy).then_inc(s_agc, 1)
                act.wait_ge(s_a0, b + 1)
                a.activation(a0_t[p][S:P, :], psum[0:S, 6, D:D + P], ACT.Copy).then_inc(s_a0c, 1)

            def gram_copies(b):
                for h in range(2):
                    act.wait_ge(s_gt, b * 2 + h + 2)
                    a.activation(gram_t[h], psum[:, 4 + h, :], ACT.Copy).then_inc(s_gtc, 1)

            def deviation(b):
                act.wait_ge(s_var, b + 1)
                a.activation(std, moments[:, 1:2], ACT.Sqrt).then_inc(s_std, 1)

            ahead(0, 0)
            ahead(1, 1)
            gram_copies(0)
            ahead(2, 0)
            deviation(0)
            with act.Fori(1, NU // 2) as i:
                for p in range(2):
                    b = i * 2 + p
                    gram_copies(b - 1)
                    ahead(b + 1, 1 - p)
                    deviation(b - 1)
            gram_copies(NU - 1)
            deviation(NU - 1)

        @block.vector
        def _(dve):
            v = nc.vector
            for t, w in ((row_i, NB * P), (col_i, 0)):
                last = v.memset(t[:, REST:COLS], w)
            v.memset(attr_s[:, REST:COLS, :], 0.0).then_inc(s_pad, 1)
            v.memset(empty, 0.0).then_inc(s_empty, 1)
            dve.wait_ge(s_empty, 1)
            v.memset(empty[:, :, 5], -1.0).then_inc(s_empty, 2)
            dve.wait_ge(s_edges, 64)
            v.tensor_scalar(slot.bitcast(I32), row_i, BITS, None, ALU.arith_shift_right).then_inc(s_v, 1)
            dve.wait_ge(s_v, 1)
            v.tensor_copy(block_b, slot.bitcast(I32)).then_inc(s_v, 1)
            v.tensor_scalar(row_i, row_i, P - 1, None, ALU.bitwise_and).then_inc(s_v, 1)
            dve.wait_ge(s_v, 3)
            dve.wait_ge(s_const, CONSTS)
            with dve.Fori(0, NK) as k:
                dve.wait_ge(s_count, k + 1)
                v.tensor_scalar(junk, block_b, bucket_no[:, ds(k, 1)], 0.0, ALU.is_equal, ALU.add,
                                accum_out=count[:, ds(k, 1)]).then_inc(s_count, 1)
            dve.wait_ge(s_prefix, 1)
            v.tensor_copy(total_i, psum[:, 0, 0:NK]).then_inc(s_v, 1)
            dve.wait_ge(s_v, 4)
            v.tensor_scalar(total_i, total_i, SUPER - 1, None, ALU.add).then_inc(s_v, 1)
            dve.wait_ge(s_v, 5)
            v.tensor_scalar(total_i, total_i, SHIFT, None, ALU.arith_shift_right).then_inc(s_v, 1)
            dve.wait_ge(s_v, 6)
            v.tensor_copy(groups_f, total_i).then_inc(s_v, 1)
            dve.wait_ge(s_v, 7)
            v.tensor_tensor_scan(first_group, ones_mat[:, 0:NK], groups_f, 0.0, ALU.mult, ALU.add).then_inc(s_v, 1)
            dve.wait_ge(s_v, 8)
            v.tensor_tensor(first_group, first_group, groups_f, ALU.subtract).then_inc(s_start, 1)
            dve.wait_ge(s_start, 1)
            v.tensor_scalar(before, psum[:, 0, NK:2 * NK], -1.0, None, ALU.add).then_inc(s_v, 1)
            dve.wait_ge(s_v, 9)
            v.scalar_tensor_tensor(out=before, in0=first_group, scalar=float(SUPER), in1=before,
                                   op0=ALU.mult, op1=ALU.add).then_inc(s_v, 1)
            dve.wait_ge(s_startT, 1)
            v.tensor_copy(first_col[0:NK, :], psum[0:NK, 1, 0:1]).then_inc(s_v, 1)
            dve.wait_ge(s_v, 11)
            v.tensor_scalar(started[0:NK, :], group_no[0:NK, :], first_col[0:NK, 0:1], None, ALU.is_ge).then_inc(s_began, 1)
            dve.wait_ge(s_gb, 1)
            v.tensor_scalar(group_bucket[:, :], psum[:, 2, 0:GROUPS], -1.0, None, ALU.add).then_inc(s_v, 1)
            for c, (step0, steps) in enumerate(chunks):
                width = steps * STEP
                cols = slice(step0 * STEP, step0 * STEP + width)
                with dve.Fori(0, NK // 2) as k:
                    n = k * 8 + c * 4 * NK + 1
                    dve.wait_ge(s_scan, n)
                    for h in range(2):
                        v.tensor_scalar(same[h][:, 0:width], block_b[:, cols], bucket_no[:, ds(k * 2 + h, 1)], None, ALU.is_equal).then_inc(s_scan, 1)
                    for h in range(2):
                        dve.wait_ge(s_scan, n + 1 + h)
                        v.tensor_tensor_scan(scan[h][:, 0:width], ones_row[:, 0:width], same[h][:, 0:width], before[:, ds(k * 2 + h, 1)], ALU.mult, ALU.add).then_inc(s_scan, 1)
                    for h in range(2):
                        dve.wait_ge(s_scan, n + 3 + 3 * h)
                        dve.sem_inc(s_passed, 1)
                        v.tensor_copy(before[:, ds(k * 2 + h, 1)], scan[h][:, width - 1:width]).then_inc(s_scan, 1)
                        v.copy_predicated(slot[:, cols], same[h][:, 0:width], scan[h][:, 0:width]).then_inc(s_scan, 1)
                dve.wait_ge(s_scan, (c + 1) * 4 * NK + 1)
                v.engine_nop().then_inc(s_slots, steps)
            v.memset(sums[:, :, :], 0.0).then_inc(s_sums0, 1)
            dve.wait_ge(s_sums0, 1)
            v.engine_nop().then_inc(s_free, RING)

            def features(i, r):
                dve.wait_ge(s_xg[r], i * 16 * LANE + 16 * LANE)
                s_part = xx[r][:, :, 0:S]
                v_part = xx[r][:, :, S:D].rearrange("p j (u i) -> p j u i", i=3)
                v.tensor_tensor(vprod[r].rearrange("p j (u i) -> p j u i", i=3), v_part,
                                spread(rec[r][:, :, 0:3], 2, V), ALU.mult).then_inc(s_vp, 1)
                v.tensor_tensor(xr[r][:, :, 0:3 * S].rearrange("p j (i u) -> p j i u", u=S), spread(s_part, 2, 3),
                                spread(rec[r][:, :, 0:3], 3, S), ALU.mult)
                v.tensor_tensor(hot[r], spread(iota[:, :], 1, LANE), spread(rec[r][:, :, 5], 2, P), ALU.is_equal)
                dve.wait_ge(s_vp, i * RING + r + 1)
                v.tensor_reduce(xr[r][:, :, 3 * S:3 * S + V], vprod[r].rearrange("p j (u i) -> p j u i", i=3), AX_X,
                                ALU.add).then_inc(s_xr, 1)

            def add_group(q, r):
                bucket = dve.value_load(group_bucket[0:1, ds(q, 1)], min_val=0, max_val=NK - 1)
                dve.wait_ge(s_grp, q + 1)
                dve.wait_ge(s_free, q + RING)
                to = sums[:, ds(bucket, 1), :].rearrange("p o c -> p (o c)")
                bank = 2 * (r % 2)
                v.tensor_tensor(to[:, 0:SUMS_A], to[:, 0:SUMS_A], psum[:, bank, 0:SUMS_A], ALU.add)
                v.tensor_tensor(to[:, SUMS_A:SUMS], to[:, SUMS_A:SUMS], psum[:, bank + 1, 0:SUMS - SUMS_A], ALU.add).then_inc(s_free, 1)

            for r in range(RING):
                features(0, r)
                if r:
                    add_group(r - 1, r - 1)
            with dve.Fori(1, GROUPS // RING) as i:
                for r in range(RING):
                    features(i, r)
                    add_group(i * RING + r - 1, (r - 1) % RING)
            add_group(GROUPS - 1, RING - 1)

            dve.wait_ge(s_free, GROUPS + RING)
            for t in w_msg + w_lin:
                last = v.memset(t, 0.0)
            last.then_inc(s_w, 1)
            v.engine_nop().then_inc(s_zfree, ZRING)
            dve.wait_ge(s_wready, 1)

            def finish(b, p):
                dve.wait_ge(s_u, b + 1)
                v.tensor_tensor(y2, psum[:, 6, D + P:2 * D + P], rr[p], ALU.add).then_inc(s_y, 1)
                yield
                dve.wait_ge(s_y, b * 5 + 1)
                v.tensor_tensor(y1[p][:, 0:S], y1[p][:, 0:S], y2[:, 0:S], ALU.add)
                y1v = y1[p][:, S:D].rearrange("p (w i) -> p i w", i=3)
                v.tensor_tensor(y1v, y1v, y2[:, S:D].rearrange("p (i w) -> p i w", i=3), ALU.add).then_inc(s_y, 1)
                yield
                dve.wait_ge(s_y, b * 5 + 2)
                v.bn_stats(stats, y1[p]).then_inc(s_y, 1)
                yield
                dve.wait_ge(s_y, b * 5 + 3)
                dve.sem_inc(s_passed, 1)
                v.bn_aggr(moments, stats).then_inc(s_y, 1)
                yield
                dve.wait_ge(s_y, b * 5 + 4)
                v.tensor_scalar(moments[:, 1:2], moments[:, 1:2], EPS, None, ALU.add).then_inc(s_var, 1)
                yield
                dve.wait_ge(s_std, b + 1)
                v.reciprocal(rstd, std).then_inc(s_y, 1)
                yield
                dve.wait_ge(s_y, b * 5 + 5)
                v.tensor_scalar(xall[:, ds(b, 1), :].rearrange("p o c -> p (o c)"), y1[p], moments[:, 0:1], rstd, ALU.subtract,
                                ALU.mult).then_inc(s_done, 1)

            def update(b, p, ending):
                a0 = agg[p][:, 0:S]
                a1 = agg[p][:, S:D].rearrange("p (i v) -> p i v", i=3)
                xv = blk_x[p][:, S:D].rearrange("p (u i) -> p i u", i=3)
                pu = prod_u.rearrange("p (i w k) -> p i w k", i=3, k=2 * V)
                rr0, rr1 = rr[p][:, 0:S], rr[p][:, S:D].rearrange("p (i w) -> p i w", w=V)
                VB, W1 = BANK // S, BANK // V
                dve.wait_ge(s_agc, b + 1)
                dve.wait_ge(s_main, b + 1)
                for z, what in enumerate(ORDER):
                    n, kind = what[1], what[0]
                    bank = psum[:, z % ZRING, :]
                    if kind == "s":
                        if n >= 4:
                            dve.wait_ge(s_psum, b * PAIRS + n // 2 - 1)
                        dve.wait_ge(s_z, b * ZALL + z + 1)
                        v.tensor_tensor(prod_ss[n % 4].rearrange("p (v w) -> p v w", w=S), bank.rearrange("p (v w) -> p v w", w=S),
                                        spread(a0[:, n * VB:(n + 1) * VB], 2, S), ALU.mult).then_inc(s_zfree, 1)
                    else:
                        k = what[2]
                        if n and k == 0:
                            dve.wait_ge(s_red, b + 1)
                        dve.wait_ge(s_z, b * ZALL + z + 1)
                        for m in range(3):
                            last = v.tensor_tensor(pu[:, m, :, k * V:(k + 1) * V], bank.rearrange("p (w k) -> p w k", k=V),
                                                   spread((xv if k else a1)[:, m], 1, W1), ALU.mult)
                        last.then_inc(s_zfree, 1)
                        if n and k:
                            v.tensor_scalar(y1[p], blk_x[p], 2.0, None, ALU.mult)
                            dve.wait_ge(s_psum, (b + 1) * PAIRS)
                            v.tensor_reduce(rr0, psum[:, 7, :].rearrange("p (v w) -> p w v", w=S), AX_X, ALU.add)
                        if k:
                            dve.wait_ge(s_zfree, b * ZALL + ZRING + z + 1)
                            v.tensor_reduce(rr1[:, :, n * W1:(n + 1) * W1], pu, AX_X, ALU.add).then_inc(s_main if n else s_red, 1)
                    if z > 4:
                        next(ending, None)

            update(0, 0, iter(()))
            update(1, 1, finish(0, 0))
            with dve.Fori(1, NU // 2) as i:
                update(i * 2, 0, finish(i * 2 - 1, 1))
                update(i * 2 + 1, 1, finish(i * 2, 0))
            dve.wait_ge(s_main, NU + 1)
            for _ in finish(NU - 1, 1):
                pass

        @block.tensor
        def _(pe):
            t = nc.tensor
            pe.wait_ge(s_const, CONSTS)
            pe.wait_ge(s_count, NK + 1)
            t.matmul(psum[:, 0, 0:NK], ones_mat, count, start=True, stop=True)
            t.matmul(psum[:, 0, NK:2 * NK], lower, count, start=True, stop=True).then_inc(s_prefix, 1)
            pe.wait_ge(s_start, 1)
            t.transpose(psum[0:NK, 1, 0:P], first_group, ident[:, :]).then_inc(s_startT, 1)
            pe.wait_ge(s_began, 1)
            t.matmul(psum[:, 2, 0:GROUPS], ones_mat[0:NK, :], started[0:NK, :], start=True, stop=True).then_inc(s_gb, 1)

            with pe.Fori(0, GROUPS // RING) as i:
                for r in range(RING):
                    q = i * RING + r
                    bank = 2 * (r % 2)
                    pe.wait_ge(s_xr, q + 1)
                    pe.wait_ge(s_xd, q + 1)
                    pe.wait_ge(s_free, q + RING - 1)
                    for j in range(LANE):
                        first, end = j == 0, j == LANE - 1
                        t.matmul(psum[:, bank, 0:SUMS_A], hot[r][:, j, :], xx[r][:, j, :], start=first, stop=end, skip_group_check=True)
                        last = t.matmul(psum[:, bank + 1, 0:SUMS - SUMS_A], hot[r][:, j, :], xr[r][:, j, :], start=first, stop=end,
                                        skip_group_check=True)
                    last.then_inc(s_grp, 1)

            pe.wait_ge(s_wready, 1)
            turned = [(P, 2 * D, 5, 2 * P, 0), (S, 0, 5, 0, P), (S, D, 5, P, 2 * P), (3 * V, S, 4, 0, 3 * P),
                      (3 * V, D + S, 4, P, 4 * P), (3 * V, 2 * D + 2 * S, 4, 2 * P, 5 * P)]
            weight_of = [4, 0, 2, 1, 3, 5]

            def turn(b, p):
                pe.wait_ge(s_blk, b + 1)
                for rows, c, bank, to, _ in turned:
                    t.transpose(psum[0:rows, bank, to:to + P], blk_sum[:, c:c + rows], ident[:, :])
                t.transpose(psum[0:S, 5, 3 * P:4 * P], blk_x[p][:, 0:S], ident[:, :])
                t.transpose(psum[0:3 * V, 4, 3 * P:4 * P], blk_x[p][:, S:D], ident[:, :]).then_inc(s_t, 1)

            def messages(b, p):
                pe.wait_ge(s_tt, b + 1)
                for n, (rows, _, _, _, at) in enumerate(turned):
                    last = t.matmul(psum[:, 6, 0:D], flip[0:rows, at:at + P], w_msg[weight_of[n]][0:rows, :],
                                    start=(n == 0), stop=(n == len(turned) - 1), skip_group_check=True)
                last.then_inc(s_ag, 1)

            def turn_a0(b, p):
                pe.wait_ge(s_const, CONSTS)
                pe.wait_ge(s_agc, b + 1)
                t.transpose(psum[0:S, 6, D:D + P], agg[p][:, 0:S], ident[:, :]).then_inc(s_a0, 1)

            def products(b, p, z0, z1):
                for z in range(z0, z1):
                    pe.wait_ge(s_zfree, b * ZALL + z + 1)
                    what = ORDER[z]
                    n = what[1]
                    if what[0] == "s":
                        lhs, rhs = (xs_high if n % 2 else xs_low)[p], w_ss[:, n // 2 * BANK:(n // 2 + 1) * BANK]
                    else:
                        if what[2]:
                            pe.wait_ge(s_a0c, b + 1)
                        lhs, rhs = (a0_t if what[2] else xs_low)[p], w_u1[:, n * BANK:(n + 1) * BANK]
                    t.matmul(psum[:, z % ZRING, :], lhs, rhs, start=True, stop=True).then_inc(s_z, 1)

            def sum_pair(b, k):
                if k == 0:
                    pe.wait_ge(s_main, b + 1)
                pe.wait_ge(s_pair, b * PAIRS + k + 1)
                t.matmul(psum[:, 7, :], ident[:, :], prod_ss[2 * k % 4], start=(k == 0), stop=(k == PAIRS - 1)).then_inc(s_psum, 1)

            def turn_gram(b):
                pe.wait_ge(s_g, b * 5 + 5)
                for c in range(8):
                    last = t.transpose(psum[:, 4 + c // 4, c % 4 * P:c % 4 * P + P], gram[:, c * P:(c + 1) * P], ident[:, :])
                    if c % 4 == 3:
                        last.then_inc(s_gt, 1)

            def other_terms(b, p, last_block=False):
                if not last_block:
                    pe.wait_ge(s_a0c, b + 2)
                pe.wait_ge(s_gtc, b * 2 + 3)
                to = psum[:, 6, D + P:2 * D + P]
                t.matmul(to, xs_low[p], w_lin[0], start=True, stop=False, skip_group_check=True)
                t.matmul(to, xv_t[p][0:3 * V, :], w_lin[1][0:3 * V, :], start=False, stop=False, skip_group_check=True)
                for c in range(8):
                    last = t.matmul(to[:, 0:S], gram_t[c // 4][:, c % 4 * P:c % 4 * P + P], w_vv[:, c, :],
                                    start=False, stop=(c == 7), skip_group_check=True)
                last.then_inc(s_u, 1)

            def block_(b, p, before=True):
                products(b, p, 0, 4)
                if before:
                    turn_gram(b - 1)
                products(b, p, 4, 5)
                sum_pair(b, 0)
                products(b, p, 5, 6)
                if before:
                    other_terms(b - 1, 1 - p)
                sum_pair(b, 1)
                products(b, p, 6, 7)
                turn(b + 1, 1 - p)
                products(b, p, 7, 9)
                if before:
                    pe.wait_ge(s_y, (b - 1) * 5 + 1)
                messages(b + 1, 1 - p)
                products(b, p, 9, 10)
                sum_pair(b, 2)
                products(b, p, 10, 11)
                turn_a0(b + 1, 1 - p)
                sum_pair(b, 3)
                products(b, p, 11, ZALL)

            turn(0, 0)
            messages(0, 0)
            turn_a0(0, 0)
            block_(0, 0, False)
            block_(1, 1)
            with pe.Fori(1, NU // 2) as i:
                block_(i * 2, 0)
                block_(i * 2 + 1, 1)
            turn_gram(NU - 1)
            other_terms(NU - 1, 1, True)


_INS = ['x', 'src', 'dst', 'edge_attr_4', 'node_vec1', 'L0_gnn_Wm_ss', 'L0_gnn_Wm_vv', 'L0_gnn_Wm_sv', 'L0_gnn_Wm_vs',
        'L0_gnn_Lm_s', 'L0_gnn_Lm_v', 'L0_gnn_Wu_ss', 'L0_gnn_Wu_vv', 'L0_gnn_Wu_sv', 'L0_gnn_Wu_vs', 'L0_gnn_Lu_s',
        'L0_gnn_Lu_v']


def kernel(**inputs):
    import numpy as _np
    import concourse.bacc as _bacc
    from concourse import mybir as _mybir
    from concourse.bass_utils import run_bass_kernel_spmd as _run

    nc = _bacc.Bacc("TRN2", target_bir_lowering=False, num_devices=1)
    arrays, args = {}, []
    for name in _INS:
        a = _np.ascontiguousarray(inputs[name])
        arrays[f"in_{name}_dram"] = a
        args.append(nc.dram_tensor(f"in_{name}_dram", a.shape, _mybir.dt.from_np(a.dtype), kind="ExternalInput").ap())
    out = nc.dram_tensor("out_0_dram", inputs['x'].shape, _mybir.dt.float32, kind="ExternalOutput").ap()
    gnn_kernel(nc, *args, out)
    r = _run(nc, [arrays], core_ids=[0])
    return r.results[0]["out_0_dram"]
```

```python
from contextlib import ExitStack

import concourse.bass as bass
from concourse import mybir

P = 128
LANE = 4
HALF = LANE // 2
SUPER = P * HALF
SHIFT = SUPER.bit_length() - 1
BITS = P.bit_length() - 1
STEP = 13
FIRST_STEPS = (5, 12)
CHUNK_STEPS = 27
REC = 6
RING = 4
S, V = 64, 32
D = S + 3 * V
SR, VR = 2 * D, 2 * D + 3 * S
SUMS = VR + V
SUMS_A = SUMS // 2
BANK = 512
ZSS, ZU = S * S // BANK, V * V // BANK
PAIRS = ZSS // 2
SRING = URING = 2
PAIR_AT = (0, 1, 2, 1)
PRODS = 4
REGION = 17752
EPS = 1e-5
INV_SQRT3, INV8, INV_SQRT32 = 0.5773502691896258, 0.125, 0.17677669529663687
INV64, INV32, INV_SQRT2048 = 0.015625, 0.03125, 0.022097086912079608

ALU = mybir.AluOpType
ACT = mybir.ActivationFunctionType
F32, BF16 = mybir.dt.float32, mybir.dt.bfloat16
I32, U32, U16 = mybir.dt.int32, mybir.dt.uint32, mybir.dt.uint16
AX_X = mybir.AxisListType.X
ds = bass.ds


def spread(ap, axis, n):
    ap = ap.unsqueeze(axis)
    shape = list(ap.shape)
    shape[axis] = n
    return ap.to_broadcast(shape)


def gnn_kernel(nc, x, src, dst, attr, node_vec, Wm_ss, Wm_vv, Wm_sv, Wm_vs, Lm_s, Lm_v,
               Wu_ss, Wu_vv, Wu_sv, Wu_vs, Lu_s, Lu_v, out):
    N, E = x.shape[0], src.shape[0]
    NB = -(-N // P)
    NK = NB + 1 + (NB + 1) % 2
    PAIRS_OF_BLOCKS = NB // 2
    NTAIL = N - (NB - 1) * P
    STEPS = -(-(-(-E // P)) // STEP)
    STEPS += STEPS % 2
    COLS = STEPS * STEP
    CHUNK = CHUNK_STEPS * STEP
    chunks = []
    while not chunks or sum(chunks[-1]) < STEPS:
        at = sum(chunks[-1]) if chunks else 0
        n = FIRST_STEPS[len(chunks)] if len(chunks) < len(FIRST_STEPS) else CHUNK_STEPS
        chunks.append((at, min(n, STEPS - at)))
    FULL = E // COLS
    REST = E - FULL * COLS
    assert FULL == P - 1 and 0 < REST < COLS and NB % 2 == 1 and NB > 3
    GROUPS = -(-(P * COLS // SUPER + NK) // (2 * RING)) * 2 * RING
    BATCHES = GROUPS // 2
    assert GROUPS % 2 == 0 and GROUPS // 2 <= BANK and NB <= BATCHES // RING
    SLOTS = GROUPS * SUPER

    table = nc.dram_tensor("edge_table", (SLOTS, REC), F32, kind="Internal").ap()
    batches_of_table = table.rearrange("(q h p j) w -> q p h (j w)", h=2, p=P, j=HALF)

    ctx = ExitStack()
    with ctx:
        def sb(name, shape, dt=F32):
            return ctx.enter_context(nc.sbuf_tensor(name, shape, dt))

        def sem(name):
            return ctx.enter_context(nc.semaphore(name))

        xall = sb("xall", [P, NB + 1, D])
        sums = sb("sums", [P, NK, SUMS])
        residual = xall[:, NB, :]
        ident = sb("ident", [P, P])
        iota = sb("iota", [P, P])
        region = sb("region", [P, REGION])

        place = [0]

        def carve(shape, dt=F32):
            n = 1
            for d in shape:
                n *= d
            words = n if dt in (F32, I32, U32) else -(-n // 2)
            v = region[:, place[0]:place[0] + words]
            place[0] += -(-words // 8) * 8
            assert place[0] <= REGION, place[0]
            if dt is not F32:
                v = v.bitcast(dt)[:, 0:n]
            if len(shape) == 2:
                v = v.rearrange("p (a b) -> p a b", b=shape[1])
            if len(shape) == 3:
                v = v.rearrange("p (a b c) -> p a b c", b=shape[1], c=shape[2])
            return v

        group_bucket = region[:, REGION - GROUPS:REGION].bitcast(I32)

        row_i = carve([COLS], I32)
        col_i = carve([COLS], I32)
        attr_s = carve([COLS, 4])
        block_b = carve([COLS], BF16)
        slot = carve([COLS])
        ones_row = carve([CHUNK])
        same = [carve([CHUNK], U16) for _ in range(2)]
        scan = [carve([CHUNK]) for _ in range(2)]
        junk = [slot.bitcast(BF16)[:, h * COLS:(h + 1) * COLS] for h in range(2)]
        FILL = SLOTS // P // 16
        assert FILL * 16 * P == SLOTS
        W0 = FIRST_STEPS[0] * STEP
        in_sums = sums[:, :, :].rearrange("p b c -> p (b c)")
        first_same, first_keep, first_scan = [in_sums[:, n * NK * (W0 + 1):(n + 1) * NK * (W0 + 1)] for n in range(3)]
        raw_u1 = xall[:, :, :].rearrange("p b d -> p (b d)")[:, 0:V * V]
        empty = carve([FILL, REC])
        bucket_no = carve([NK])
        count = carve([NK])
        total_i = carve([NK], I32)
        groups_f = carve([NK])
        first_group = carve([NK])
        before = carve([NK])
        ones_mat = carve([P])
        lower = carve([P])
        first_col = carve([1])
        group_no = carve([GROUPS])
        started = carve([GROUPS])
        stage_rec = [carve([STEP, REC]) for _ in range(2)]
        stage_slot = [carve([STEP], I32) for _ in range(2)]

        assert place[0] <= REGION - GROUPS, place[0]

        place[0] = 0
        rec = [carve([LANE, REC]) for _ in range(RING)]
        feat = [carve([LANE, SUMS]) for _ in range(RING)]
        hot = [carve([LANE, P]) for _ in range(RING)]
        vprod = [carve([LANE, 3 * V]) for _ in range(RING)]

        WEIGHTS = S * S // 2 + V * V + V * V // P * S + 4 * D + 3 * V
        AT_WEIGHTS = REGION - GROUPS - WEIGHTS
        assert place[0] <= AT_WEIGHTS, place[0]
        place[0] = AT_WEIGHTS
        w_ss = carve([S * S // 2])
        w_u1 = carve([V * V])
        w_vv = carve([V * V // P, S])
        w_lm = carve([D])
        w_wm = carve([D])
        w_sv01 = carve([3 * V])
        w_sv2 = carve([D])
        w_lin = carve([D])
        assert place[0] == REGION - GROUPS
        flip = carve([6 * P])
        stats = carve([6])
        moments = carve([2])
        std = carve([1])
        rstd = carve([1])
        place[0] = 0
        blk_sum = carve([SUMS])
        blk_x = [carve([D]) for _ in range(2)]
        xs_low = [carve([P]) for _ in range(2)]
        xs_high = [carve([P]) for _ in range(2)]
        xv_t = [carve([P]) for _ in range(2)]
        agg = [carve([D]) for _ in range(2)]
        a0_t = [carve([P]) for _ in range(2)]
        gram = carve([V * V])
        gram_t = [carve([BANK]) for _ in range(2)]
        gtmp = carve([V * V])
        rr = [carve([D]) for _ in range(2)]
        y = [carve([D]) for _ in range(2)]
        prod_ss = [carve([BANK]) for _ in range(PRODS)]
        pair = [carve([BANK]) for _ in range(3)]
        prod_u = carve([3 * (BANK // V) * 2 * V])
        assert place[0] <= AT_WEIGHTS, place[0]

        psum = ctx.enter_context(nc.psum_tensor("psum", [P, 8, BANK], F32))

        s_passed = sem("wait_passed")
        s_pad = sem("edge_pads_cleared")
        s_edges = sem("edges_loaded")
        s_attr = sem("attributes_loaded")
        s_x = sem("x_loaded")
        s_const = sem("constants_ready")
        s_empty = sem("empty_records_ready")
        s_table = sem("table_cleared")
        s_v = sem("vector_chain")
        s_count = sem("edges_counted")
        s_prefix = sem("prefixes_ready")
        s_start = sem("group_starts_ready")
        s_startT = sem("group_starts_turned")
        s_began = sem("started_ready")
        s_gb = sem("group_buckets_summed")
        s_slots = sem("slots_ready")
        s_scan = sem("scan_chain")
        s_staged = sem("records_staged")
        s_scattered = [sem(f"records_scattered{h}") for h in range(2)]
        s_first = sem("first_piece_chain")
        s_sums0 = sem("sums_cleared")
        s_rec = [sem(f"records_loaded{r}") for r in range(RING)]
        s_xg = [sem(f"x_gathered{r}") for r in range(RING)]
        s_xd = sem("x_times_dist_ready")
        s_vp = sem("v_products_ready")
        s_xr = sem("edge_features_ready")
        s_grp = sem("group_summed")
        s_added = sem("groups_added")
        s_w = sem("weights_cleared")
        s_raw = sem("raw_weight_loaded")
        s_turned = sem("raw_weight_reordered")
        s_wload = sem("weights_loaded")
        s_wready = sem("weights_ready")
        s_blk = sem("block_staged")
        s_t = sem("block_turned")
        s_tt = sem("turned_block_copied")
        s_ag = sem("messages_summed")
        s_agc = sem("messages_copied")
        s_a0 = sem("a0_turned")
        s_a0c = sem("a0_turned_copied")
        s_zs = sem("u0_bank_ready")
        s_sfree = sem("u0_banks_used")
        s_zu = sem("u1_bank_ready")
        s_ufree = sem("u1_banks_used")
        s_pair = sem("u0_pairs_added")
        s_half = sem("first_pairs_summed")
        s_tree = sem("u0_tree_chain")
        s_red = sem("products_reduced")
        s_g = sem("gram_chain")
        s_gt = sem("gram_turned")
        s_gtc = sem("gram_turned_copied")
        s_u = sem("update_summed")
        s_main = sem("block_products_done")
        s_y = sem("norm_chain")
        s_var = sem("variance_ready")
        s_std = sem("deviation_ready")
        s_done = sem("block_done")
        s_store = sem("stored")

        CONSTS = 11

        block = ctx.enter_context(nc.Block())

        def weight_loads():
            for h in range(2):
                yield (w_ss[h * S:h * S + S, :].rearrange("p (z k) -> p z k", k=BANK),
                       Wu_ss.rearrange("u v w -> u (v w)").rearrange("u (z h k) -> u z h k", h=2, k=BANK)[:, :, h, :])
            yield w_vv, Wu_vv.rearrange("u v w -> (u v) w").rearrange("(c p) w -> p c w", p=P)
            yield w_lm[0:S, 0:S], Lm_s
            yield w_wm[0:S, 0:S], Wm_ss
            for i in range(2):
                yield w_sv01[S * i:S * i + S, V * i:V * i + V], Wm_sv
            yield w_sv2[0:S, S + 2 * V:D], Wm_sv
            yield w_sv2[S:S + V, 0:S], Wm_vv
            yield w_lin[0:S, 0:S], Lu_s
            for i in range(3):
                c = slice(S + V * i, S + V * i + V)
                yield w_lm[i:3 * V:3, c], Lm_v
                yield w_wm[i:3 * V:3, c], Wm_vs
                yield w_lin[i:3 * V:3, c], Lu_v

        WLOADS = len(list(weight_loads()))

        @block.sync
        def _(sp):
            sp.sem_inc(s_count, 2)
            for s in (s_scan, s_gt, s_gtc, s_main, s_done):
                sp.sem_inc(s, 1)
            sp.wait_ge(s_pad, 1)
            for tile_, dram in ((row_i, src), (col_i, dst)):
                sp.dma_start(tile_[0:FULL, :], dram[0:FULL * COLS].rearrange("(p t) -> p t", t=COLS)).then_inc(s_edges, 16)
                sp.dma_start(tile_[FULL:P, 0:REST], dram[FULL * COLS:E].rearrange("(p t) -> p t", p=1)).then_inc(s_edges, 16)
            sp.dma_start(attr_s[0:FULL, :, :], attr[0:FULL * COLS, :].rearrange("(p t) w -> p t w", t=COLS)).then_inc(s_attr, 16)
            sp.dma_start(attr_s[FULL:P, 0:REST, :], attr[FULL * COLS:E, :].rearrange("(p t) w -> p t w", p=1)).then_inc(s_attr, 16)
            sp.wait_ge(s_empty, 3)
            rows = SLOTS // P
            flat = table.rearrange("(p r) w -> p r w", r=rows)
            for c in range(rows // FILL):
                sp.dma_start(flat[:, c * FILL:(c + 1) * FILL, :], empty).then_inc(s_table, 16)
            with nc.allow_non_contiguous_dma(reason="small weights"):
                sp.dma_start(raw_u1[0:S, :], Wu_sv.rearrange("u v w -> u (v w)")).then_inc(s_raw, 16)
                sp.dma_start(raw_u1[S:P, :].rearrange("p (u w) -> p u w", w=V), Wu_vs.rearrange("u v w -> v u w")).then_inc(s_raw, 16)

            for h in range(2):
                sp.wait_ge(s_scattered[h], 16 * STEP * (STEPS // 2))

            def load_records(i, first=False):
                for r in range(RING):
                    if not first:
                        sp.wait_ge(s_grp, (i - 1) * 2 * RING + 2 * r + 2)
                    sp.dma_start(rec[r].rearrange("p (h j) w -> p h (j w)", h=2),
                                 batches_of_table[ds(i * RING + r, 1)].rearrange("q p h f -> (q p) h f")).then_inc(s_rec[r], 16)

            load_records(0, first=True)
            sp.wait_ge(s_w, 1)
            with nc.allow_non_contiguous_dma(reason="small weights"):
                for to, frm in weight_loads():
                    sp.dma_start(to, frm).then_inc(s_wload, 16)
            sp.wait_ge(s_turned, 1)
            sp.wait_ge(s_const, CONSTS)
            sp.dma_start(xall[0:NTAIL, NB - 1, :], x[(NB - 1) * P:N, :]).then_inc(s_x, 16)
            with sp.Fori(1, NB) as i:
                load_records(i)
                sp.dma_start(xall[:, ds(i - 1, 1), :].rearrange("p o d -> p (o d)"), x[ds((i - 1) * P, P), :]).then_inc(s_x, 16)
            with sp.Fori(NB, BATCHES // RING) as i:
                load_records(i)

            with sp.Fori(0, PAIRS_OF_BLOCKS) as i:
                sp.wait_ge(s_done, 2 * i + 3)
                sp.dma_start(out[ds(i * 2 * P, 2 * P), :].rearrange("(b p) d -> p b d", p=P),
                             xall[:, ds(i * 2, 2), :]).then_inc(s_store, 16)
            sp.wait_ge(s_done, NB + 1)
            sp.dma_start(out[(NB - 1) * P:N, :], xall[0:NTAIL, NB - 1, :]).then_inc(s_store, 16)
            sp.wait_ge(s_store, 16 * (PAIRS_OF_BLOCKS + 1))

        @block.gpsimd
        def _(pool):
            g = nc.gpsimd
            g.iota(iota[:, :], [[1, P]], base=0, channel_multiplier=0, allow_small_or_imprecise_dtypes=True).then_inc(s_const, 1)
            g.iota(bucket_no, [[1, NK]], base=0, channel_multiplier=0, allow_small_or_imprecise_dtypes=True).then_inc(s_const, 1)
            g.iota(group_no, [[1, GROUPS]], base=0, channel_multiplier=0, allow_small_or_imprecise_dtypes=True).then_inc(s_const, 1)
            g.memset(ones_mat, 1.0).then_inc(s_const, 1)
            g.memset(ones_row, 1.0).then_inc(s_const, 1)
            pool.wait_ge(s_const, 5)
            g.affine_select(out=lower, in_=ones_mat, pattern=[[1, P]], compare_op=ALU.is_gt, fill=0.0,
                            base=0, channel_multiplier=-1).then_inc(s_const, 1)
            g.affine_select(out=ident[:, :], in_=ones_mat, pattern=[[1, P]], compare_op=ALU.is_equal, fill=0.0,
                            base=0, channel_multiplier=-1).then_inc(s_const, 1)
            g.memset(xall[:, NB - 1, :], 0.0).then_inc(s_const, 1)
            g.memset(residual[:, :], 2.0).then_inc(s_const, 1)
            pool.wait_ge(s_const, 9)
            g.affine_select(out=residual[:, 0:S], in_=residual[:, 0:S], pattern=[[-1, S]], compare_op=ALU.is_equal, fill=0.0,
                            base=0, channel_multiplier=1).then_inc(s_const, 1)
            residual_v = residual[:, S:D].rearrange("p (i w) -> p i w", i=3)
            g.affine_select(out=residual_v, in_=residual_v, pattern=[[-1, 3], [-3, V]], compare_op=ALU.is_equal, fill=0.0,
                            base=0, channel_multiplier=1).then_inc(s_const, 1)
            pool.wait_ge(s_table, 16 * (SLOTS // P // FILL))
            with pool.Fori(0, STEPS // 2) as i:
                for h in range(2):
                    pool.wait_ge(s_staged, i * 2 + h + 1)
                    pool.sem_inc(s_passed, 1)
                    for j in range(STEP):
                        g.indirect_dma_start(
                            out=table, out_offset=bass.IndirectOffsetOnAxis(ap=stage_slot[h][:, j:j + 1].bitcast(U32), axis=0),
                            in_=stage_rec[h][:, j, :], in_offset=None).then_inc(s_scattered[h], 16)
            with pool.Fori(0, BATCHES // RING) as i:
                for r in range(RING):
                    pool.wait_ge(s_rec[r], i * 16 + 16)
                    pool.sem_inc(s_passed, 1)
                    for j in range(LANE):
                        g.indirect_dma_start(
                            out=feat[r][:, j, 0:D], out_offset=None, in_=x,
                            in_offset=bass.IndirectOffsetOnAxis(ap=rec[r][:, j, 4:5].bitcast(U32), axis=0)).then_inc(s_xg[r], 16)
            def block_(b, p):
                xv = blk_x[p][:, S:D].rearrange("p (u i) -> p u i", i=3)
                a1 = agg[p][:, S:D].rearrange("p (i v) -> p i v", i=3)

                def add_pair(k):
                    if k == 0:
                        pool.wait_ge(s_tree, b * 3 + 2)
                    if k == 2:
                        pool.wait_ge(s_tree, b * 3 + 3)
                    if k == 3:
                        pool.wait_ge(s_half, b + 1)
                    pool.wait_ge(s_sfree, b * ZSS + 2 * k + 2 + SRING)
                    g.tensor_tensor(pair[PAIR_AT[k]], prod_ss[2 * k % PRODS], prod_ss[2 * k % PRODS + 1], ALU.add).then_inc(s_pair, 1)

                gm, gt = gram.rearrange("p (u v) -> p u v", v=V), gtmp.rearrange("p (u v) -> p u v", v=V)
                pool.wait_ge(s_agc, b + 1)
                pool.wait_ge(s_gt, b * 2 + 1)
                for c in range(3):
                    if c == 2:
                        add_pair(1)
                        pool.wait_ge(s_g, b * 5 + 3)
                    g.tensor_tensor(gt if c else gm, spread(xv[:, :, c], 2, V), spread(a1[:, c, :], 1, V), ALU.mult).then_inc(s_g, 1)
                    if c:
                        if c == 2:
                            pool.wait_ge(s_pair, b * PAIRS + 2 + PRODS // 2)
                            g.tensor_tensor(pair[0], pair[0], pair[1], ALU.add).then_inc(s_half, 1)
                        add_pair(2 * c - 2)
                        pool.wait_ge(s_g, b * 5 + 2 * c)
                        g.tensor_tensor(gm, gm, gt, ALU.add).then_inc(s_g, 1)
                add_pair(3)

            with pool.Fori(0, PAIRS_OF_BLOCKS) as i:
                block_(i * 2, 0)
                block_(i * 2 + 1, 1)
            block_(NB - 1, 0)

        @block.scalar
        def _(act):
            a = nc.scalar
            act.wait_ge(s_attr, 32)
            act.wait_ge(s_edges, 64)
            def stage(i, first=False):
                for h in range(2):
                    cols = ds(i * 2 * STEP + h * STEP, STEP)
                    act.wait_ge(s_slots, i * 2 + h + 1)
                    if not first:
                        act.wait_ge(s_scattered[h], i * 16 * STEP)
                    a.activation(stage_rec[h][:, :, 0:4], attr_s[:, cols, :], ACT.Copy)
                    a.activation(stage_rec[h][:, :, 4].bitcast(I32), col_i[:, cols], ACT.Copy)
                    a.activation(stage_rec[h][:, :, 5], row_i[:, cols], ACT.Copy)
                    a.activation(stage_slot[h], slot[:, cols], ACT.Copy).then_inc(s_staged, 1)

            stage(0, first=True)
            with act.Fori(1, STEPS // 2) as i:
                stage(i)
            act.wait_ge(s_raw, 32)
            act.wait_ge(s_w, 1)
            a.activation(w_u1.rearrange("p (w v) -> p w v", v=V), raw_u1.rearrange("p (v w) -> p w v", w=V), ACT.Copy,
                         scale=INV_SQRT2048).then_inc(s_turned, 1)

            def times_dist(i):
                for r in range(RING):
                    act.wait_ge(s_xg[r], i * 16 * LANE + 16 * LANE)
                    for j in range(LANE):
                        last = a.activation(feat[r][:, j, D:2 * D], feat[r][:, j, 0:D], ACT.Copy, scale=rec[r][:, j, 3:4])
                    last.then_inc(s_xd, 1)

            with act.Fori(0, BATCHES // RING // 2) as i:
                times_dist(i)
            act.wait_ge(s_wload, 16 * WLOADS)
            a.activation(w_ss, w_ss, ACT.Copy, scale=INV64)
            a.activation(w_vv, w_vv, ACT.Copy, scale=INV_SQRT3 * INV32)
            a.activation(w_sv01, w_sv01, ACT.Copy, scale=INV8)
            a.activation(w_sv2[0:S, :], w_sv2[0:S, :], ACT.Copy, scale=INV8)
            a.activation(w_sv2[S:S + V, :], w_sv2[S:S + V, :], ACT.Copy, scale=INV_SQRT3 * INV_SQRT32)
            for w in (w_lm, w_wm, w_lin):
                a.activation(w[0:S, 0:S], w[0:S, 0:S], ACT.Copy, scale=INV8)
                last = a.activation(w[0:3 * V, S:D], w[0:3 * V, S:D], ACT.Copy, scale=INV_SQRT32)
            last.then_inc(s_wready, 1)
            with act.Fori(BATCHES // RING // 2, BATCHES // RING) as i:
                times_dist(i)

            act.wait_ge(s_added, GROUPS + 2 * RING)
            act.wait_ge(s_x, 16 * NB)

            for h in range(2):
                for z in (xs_low[h][S:P, :], xs_high[h][0:S, :], a0_t[h][0:S, :]):
                    a.activation(z, ident[0:S, :], ACT.Copy, scale=0.0)

            def multiply(b, p, *banks):
                for n in banks:
                    act.wait_ge(s_pair, b * PAIRS + n // 2 + 1)
                    act.wait_ge(s_zs, b * ZSS + n + 1)
                    for k in range(BANK // S):
                        at = n * (BANK // S) + k
                        last = a.activation(prod_ss[n % PRODS][:, k * S:(k + 1) * S], psum[:, n % SRING, k * S:(k + 1) * S], ACT.Copy,
                                            scale=agg[p][:, at:at + 1])
                    last.then_inc(s_sfree, 1)

            def stage_block(b, p, first=False):
                if not first:
                    act.wait_ge(s_t, b)
                a.activation(blk_sum, sums[:, ds(b, 1), :].rearrange("p o c -> p (o c)"), ACT.Copy)
                if not first:
                    act.wait_ge(s_main, b)
                a.activation(blk_x[p], xall[:, ds(b, 1), :].rearrange("p o c -> p (o c)"), ACT.Copy).then_inc(s_blk, 1)

            def copy_turned(b, p):
                act.wait_ge(s_t, b + 1)
                a.activation(xs_low[p][0:S, :], psum[0:S, 5, 3 * P:BANK], ACT.Copy)
                a.activation(xs_high[p][S:P, :], psum[0:S, 5, 3 * P:BANK], ACT.Copy)
                a.activation(flip[:, 0:P], psum[:, 5, 2 * P:3 * P], ACT.Copy)
                a.activation(flip[0:S, P:3 * P], psum[0:S, 5, 0:2 * P], ACT.Copy)
                a.activation(flip[0:3 * V, 3 * P:6 * P], psum[0:3 * V, 4, 0:3 * P], ACT.Copy)
                a.activation(xv_t[p][0:3 * V, :], psum[0:3 * V, 4, 3 * P:BANK], ACT.Copy).then_inc(s_tt, 1)

            def copy_messages(b, p, first=False):
                act.wait_ge(s_ag, b + 1)
                if not first:
                    act.wait_ge(s_sfree, (b - 1) * ZSS + SRING)
                a.activation(agg[p], psum[:, 6, 0:D], ACT.Copy).then_inc(s_agc, 1)

            def copy_a0(b, p):
                act.wait_ge(s_a0, b + 1)
                a.activation(a0_t[p][S:P, :], psum[0:S, 6, D:D + P], ACT.Copy).then_inc(s_a0c, 1)

            def gram_copies(b):
                for h in range(2):
                    act.wait_ge(s_gt, b * 2 + h + 2)
                    a.activation(gram_t[h], psum[:, 4 + h, :], ACT.Copy).then_inc(s_gtc, 1)

            def deviation(b):
                act.wait_ge(s_var, b + 1)
                a.activation(std, moments[:, 1:2], ACT.Sqrt).then_inc(s_std, 1)

            def block_(b, p, before=True, before2=True, after=True):
                act.wait_ge(s_agc, b + 1)
                multiply(b, p, 0, 1)
                if before:
                    gram_copies(b - 1)
                multiply(b, p, 2)
                if after:
                    stage_block(b + 1, 1 - p)
                if before2:
                    deviation(b - 2)
                multiply(b, p, 3, 4)
                if after:
                    copy_turned(b + 1, 1 - p)
                multiply(b, p, 5)
                if after:
                    copy_messages(b + 1, 1 - p)
                multiply(b, p, 6)
                if after:
                    copy_a0(b + 1, 1 - p)
                multiply(b, p, 7)

            a.activation(std, ident[:, 0:1], ACT.Sqrt)
            stage_block(0, 0, first=True)
            copy_turned(0, 0)
            copy_messages(0, 0, first=True)
            copy_a0(0, 0)
            block_(0, 0, False, False)
            block_(1, 1, True, False)
            with act.Fori(1, PAIRS_OF_BLOCKS) as i:
                block_(i * 2, 0)
                block_(i * 2 + 1, 1)
            block_(NB - 1, 0, after=False)
            gram_copies(NB - 1)
            deviation(NB - 2)
            deviation(NB - 1)

        @block.vector
        def _(dve):
            v = nc.vector
            for t, w in ((row_i, NB * P), (col_i, 0)):
                v.memset(t[:, REST:COLS], w)
            v.memset(attr_s[:, REST:COLS, :], 0.0).then_inc(s_pad, 1)
            v.memset(empty, 0.0).then_inc(s_empty, 1)
            dve.wait_ge(s_empty, 1)
            v.memset(empty[:, :, 5], -1.0).then_inc(s_empty, 2)
            dve.wait_ge(s_edges, 64)
            v.tensor_scalar(slot.bitcast(I32), row_i, BITS, None, ALU.arith_shift_right).then_inc(s_v, 1)
            dve.wait_ge(s_v, 1)
            v.tensor_copy(block_b, slot.bitcast(I32)).then_inc(s_v, 1)
            v.tensor_scalar(row_i, row_i, P - 1, None, ALU.bitwise_and).then_inc(s_v, 1)
            dve.wait_ge(s_v, 3)
            dve.wait_ge(s_const, CONSTS)
            with dve.Fori(0, NK // 2) as k:
                for h in range(2):
                    dve.wait_ge(s_count, 2 * k + h + 1)
                    v.tensor_scalar(junk[h], block_b, bucket_no[:, ds(2 * k + h, 1)], 0.0, ALU.is_equal, ALU.add,
                                    accum_out=count[:, ds(2 * k + h, 1)]).then_inc(s_count, 1)
            dve.wait_ge(s_prefix, 1)
            v.tensor_copy(total_i, psum[:, 0, 0:NK]).then_inc(s_v, 1)
            dve.wait_ge(s_v, 4)
            v.tensor_scalar(total_i, total_i, SUPER - 1, None, ALU.add).then_inc(s_v, 1)
            dve.wait_ge(s_v, 5)
            v.tensor_scalar(total_i, total_i, SHIFT, None, ALU.arith_shift_right).then_inc(s_v, 1)
            dve.wait_ge(s_v, 6)
            v.tensor_copy(groups_f, total_i).then_inc(s_v, 1)
            dve.wait_ge(s_v, 7)
            v.tensor_tensor_scan(first_group, ones_mat[:, 0:NK], groups_f, 0.0, ALU.mult, ALU.add).then_inc(s_v, 1)
            dve.wait_ge(s_v, 8)
            v.tensor_tensor(first_group, first_group, groups_f, ALU.subtract).then_inc(s_start, 1)
            dve.wait_ge(s_start, 1)
            v.tensor_scalar(before, psum[:, 0, NK:2 * NK], -1.0, None, ALU.add).then_inc(s_v, 1)
            dve.wait_ge(s_v, 9)
            v.scalar_tensor_tensor(out=before, in0=first_group, scalar=float(SUPER), in1=before,
                                   op0=ALU.mult, op1=ALU.add).then_inc(s_v, 1)
            dve.wait_ge(s_startT, 1)
            v.tensor_copy(first_col[0:NK, :], psum[0:NK, 1, 0:1]).then_inc(s_v, 1)
            dve.wait_ge(s_v, 11)
            v.tensor_scalar(started[0:NK, :], group_no[0:NK, :], first_col[0:NK, 0:1], None, ALU.is_ge).then_inc(s_began, 1)
            dve.wait_ge(s_gb, 1)
            v.tensor_scalar(group_bucket.rearrange("p (h q) -> p h q", h=2), psum[:, 2:4, 0:GROUPS // 2], -1.0, None, ALU.add).then_inc(s_v, 1)
            rows0 = [t.rearrange("p (k c) -> p k c", c=W0 + 1) for t in (first_same, first_keep, first_scan)]
            same0, keep0, scan0 = rows0
            v.memset(first_keep, 1.0).then_inc(s_first, 1)
            v.tensor_tensor(same0[:, :, 1:], spread(block_b[:, 0:W0], 1, NK), spread(bucket_no, 2, W0), ALU.is_equal)
            dve.wait_ge(s_v, 10)
            v.tensor_copy(same0[:, :, 0], before)
            dve.wait_ge(s_first, 1)
            v.memset(keep0[:, :, 0], 0.0).then_inc(s_first, 1)
            dve.wait_ge(s_first, 2)
            v.tensor_tensor_scan(first_scan, first_keep, first_same, 0.0, ALU.mult, ALU.add).then_inc(s_first, 1)
            dve.wait_ge(s_first, 3)
            v.tensor_copy(before, scan0[:, :, W0])
            v.tensor_tensor(same0[:, :, 1:], same0[:, :, 1:], scan0[:, :, 1:], ALU.mult).then_inc(s_first, 1)
            dve.wait_ge(s_first, 4)
            v.tensor_reduce(slot[:, 0:W0], same0[:, :, 1:].rearrange("p k c -> p c k"), AX_X, ALU.add).then_inc(s_first, 1)
            dve.wait_ge(s_first, 5)
            v.engine_nop().then_inc(s_slots, FIRST_STEPS[0])
            for c, (step0, steps) in enumerate(chunks[1:]):
                width = steps * STEP
                cols = slice(step0 * STEP, step0 * STEP + width)
                with dve.Fori(0, NK // 2) as k:
                    n = k * 8 + c * 4 * NK + 1
                    dve.wait_ge(s_scan, n)
                    for h in range(2):
                        v.tensor_scalar(same[h][:, 0:width], block_b[:, cols], bucket_no[:, ds(k * 2 + h, 1)], None, ALU.is_equal).then_inc(s_scan, 1)
                    for h in range(2):
                        dve.wait_ge(s_scan, n + 1 + h)
                        v.tensor_tensor_scan(scan[h][:, 0:width], ones_row[:, 0:width], same[h][:, 0:width], before[:, ds(k * 2 + h, 1)], ALU.mult, ALU.add).then_inc(s_scan, 1)
                    for h in range(2):
                        dve.wait_ge(s_scan, n + 3 + 3 * h)
                        dve.sem_inc(s_passed, 1)
                        v.tensor_copy(before[:, ds(k * 2 + h, 1)], scan[h][:, width - 1:width]).then_inc(s_scan, 1)
                        v.copy_predicated(slot[:, cols], same[h][:, 0:width], scan[h][:, 0:width]).then_inc(s_scan, 1)
                dve.wait_ge(s_scan, (c + 1) * 4 * NK + 1)
                v.engine_nop().then_inc(s_slots, steps)
            v.memset(sums[:, :, :], 0.0).then_inc(s_sums0, 1)
            dve.wait_ge(s_sums0, 1)
            v.engine_nop().then_inc(s_added, 2 * RING)
            for h in range(2):
                dve.wait_ge(s_scattered[h], 16 * STEP * (STEPS // 2))
            for t in (w_lm, w_wm, w_sv01, w_sv2, w_lin):
                last = v.memset(t, 0.0)
            last.then_inc(s_w, 1)

            def batch(i, r, add=lambda h: None):
                x_dist, s_r, v_r = feat[r][:, :, 0:2 * D], feat[r][:, :, SR:VR], feat[r][:, :, VR:SUMS]
                dve.wait_ge(s_xg[r], i * 16 * LANE + 16 * LANE)
                v.tensor_tensor(vprod[r].rearrange("p j (u i) -> p j u i", i=3),
                                x_dist[:, :, S:D].rearrange("p j (u i) -> p j u i", i=3),
                                spread(rec[r][:, :, 0:3], 2, V), ALU.mult).then_inc(s_vp, 1)
                add(0)
                v.tensor_tensor(s_r.rearrange("p j (i u) -> p j i u", u=S), spread(x_dist[:, :, 0:S], 2, 3),
                                spread(rec[r][:, :, 0:3], 3, S), ALU.mult)
                v.tensor_tensor(hot[r], spread(iota[:, :], 1, LANE), spread(rec[r][:, :, 5], 2, P), ALU.is_equal)
                dve.wait_ge(s_vp, i * RING + r + 1)
                v.tensor_reduce(v_r, vprod[r].rearrange("p j (u i) -> p j u i", i=3), AX_X, ALU.add).then_inc(s_xr, 1)
                add(1)

            def add_group(q, r, h):
                bucket = dve.value_load(group_bucket[0:1, ds(2 * q + h, 1)], min_val=0, max_val=NK - 1)
                dve.wait_ge(s_grp, 2 * q + h + 1)
                dve.wait_ge(s_added, 2 * q + h + 2 * RING)
                to = sums[:, ds(bucket, 1), :].rearrange("p o (z c) -> p (o z) c", c=SUMS_A)
                bank = 4 * (r % 2) + 2 * h
                v.tensor_tensor(to, to, psum[:, bank:bank + 2, 0:SUMS_A], ALU.add).then_inc(s_added, 1)

            for r in range(RING):
                if r < 2:
                    batch(0, r)
                else:
                    batch(0, r, lambda h: add_group(r - 2, r - 2, h))
            with dve.Fori(1, BATCHES // RING) as i:
                for r in range(RING):
                    batch(i, r, lambda h: add_group(i * RING + r - 2, (r - 2) % RING, h))
            for q in (BATCHES - 2, BATCHES - 1):
                for h in range(2):
                    add_group(q, q % RING, h)

            dve.wait_ge(s_added, GROUPS + 2 * RING)
            v.engine_nop().then_inc(s_sfree, SRING)
            v.engine_nop().then_inc(s_ufree, URING)
            v.engine_nop().then_inc(s_pair, PRODS // 2)
            v.engine_nop().then_inc(s_tree, 3)
            dve.wait_ge(s_wready, 1)
            v.tensor_tensor(w_lin[0:3 * V, :], w_lin[0:3 * V, :], residual[0:3 * V, :], ALU.add).then_inc(s_wready, 1)

            def add_last_pairs(b):
                dve.wait_ge(s_pair, b * PAIRS + PAIRS + PRODS // 2)
                v.tensor_tensor(pair[2], pair[2], pair[1], ALU.add).then_inc(s_tree, 1)

            def add_halves(b):
                dve.wait_ge(s_half, b + 1)
                dve.wait_ge(s_tree, b * 3 + 4)
                v.tensor_tensor(pair[2], pair[2], pair[0], ALU.add).then_inc(s_tree, 1)

            def sum_u0(b, p):
                dve.wait_ge(s_tree, b * 3 + 5)
                v.tensor_reduce(rr[p][:, 0:S], pair[2].rearrange("p (v w) -> p w v", w=S), AX_X, ALU.add).then_inc(s_tree, 1)

            def add_terms(b, p, first=False):
                dve.wait_ge(s_tree, b * 3 + 6)
                if not first:
                    dve.wait_ge(s_done, b)
                dve.wait_ge(s_u, b + 1)
                v.tensor_tensor(y[p], psum[:, 7, 0:D], rr[p], ALU.add).then_inc(s_y, 1)

            def norm_stats(b, p):
                dve.wait_ge(s_y, b * 4 + 1)
                v.bn_stats(stats, y[p]).then_inc(s_y, 1)

            def norm_moments(b):
                dve.wait_ge(s_y, b * 4 + 2)
                dve.sem_inc(s_passed, 1)
                v.bn_aggr(moments, stats).then_inc(s_y, 1)

            def add_eps(b):
                dve.wait_ge(s_y, b * 4 + 3)
                v.tensor_scalar(moments[:, 1:2], moments[:, 1:2], EPS, None, ALU.add).then_inc(s_var, 1)

            def invert_deviation(b):
                dve.wait_ge(s_std, b + 1)
                v.reciprocal(rstd, std).then_inc(s_y, 1)

            def normalize(b, p):
                dve.wait_ge(s_y, b * 4 + 4)
                to = xall[:, ds(b, 1), :].rearrange("p o c -> p (o c)")
                v.tensor_scalar(to[:, 0:S], y[p][:, 0:S], moments[:, 0:1], rstd, ALU.subtract, ALU.mult)
                v.tensor_scalar(to[:, S:D].rearrange("p (w i) -> p i w", i=3), y[p][:, S:D].rearrange("p (i w) -> p i w", i=3),
                                moments[:, 0:1], rstd, ALU.subtract, ALU.mult).then_inc(s_done, 1)

            def multiply_u1(b, p, z):
                k = z % 2
                other = blk_x[p][:, S:D].rearrange("p (u i) -> p i u", i=3) if k else \
                    agg[p][:, S:D].rearrange("p (i v) -> p i v", i=3)
                to = prod_u.rearrange("p (i w k) -> p i w k", i=3, k=2 * V)[:, :, :, k * V:(k + 1) * V]
                dve.wait_ge(s_zu, b * 2 * ZU + z + 1)
                for i in range(3):
                    last = v.tensor_tensor(to[:, i], psum[:, 2 + z % URING, :].rearrange("p (w k) -> p w k", k=V),
                                           spread(other[:, i], 1, BANK // V), ALU.mult)
                last.then_inc(s_ufree, 1)

            def reduce_u1(b, p, n, signal):
                rr1 = rr[p][:, S:D].rearrange("p (i w) -> p i w", w=V)
                W1 = BANK // V
                dve.wait_ge(s_ufree, b * 2 * ZU + URING + 2 * n + 2)
                v.tensor_reduce(rr1[:, :, n * W1:(n + 1) * W1], prod_u.rearrange("p (i w k) -> p i w k", i=3, k=2 * V), AX_X,
                                ALU.add).then_inc(signal, 1)

            def block_(b, p, before=True, before2=True):
                c, cp = b - 1, 1 - p
                dve.wait_ge(s_agc, b + 1)
                dve.wait_ge(s_main, b + 1)
                multiply_u1(b, p, 0)
                if before2:
                    norm_moments(b - 2)
                if before:
                    add_last_pairs(c)
                multiply_u1(b, p, 1)
                if before2:
                    add_eps(b - 2)
                if before:
                    add_halves(c)
                reduce_u1(b, p, 0, s_red)
                if before:
                    sum_u0(c, cp)
                dve.wait_ge(s_red, b + 1)
                multiply_u1(b, p, 2)
                if before2:
                    invert_deviation(b - 2)
                multiply_u1(b, p, 3)
                if before2:
                    normalize(b - 2, p)
                if before:
                    add_terms(c, cp, not before2)
                reduce_u1(b, p, 1, s_main)
                if before:
                    norm_stats(c, cp)

            block_(0, 0, False, False)
            block_(1, 1, True, False)
            with dve.Fori(1, PAIRS_OF_BLOCKS) as i:
                block_(i * 2, 0)
                block_(i * 2 + 1, 1)
            block_(NB - 1, 0)
            norm_moments(NB - 2)
            add_eps(NB - 2)
            invert_deviation(NB - 2)
            normalize(NB - 2, 1)
            dve.wait_ge(s_main, NB + 1)
            add_last_pairs(NB - 1)
            add_halves(NB - 1)
            sum_u0(NB - 1, 0)
            add_terms(NB - 1, 0)
            norm_stats(NB - 1, 0)
            norm_moments(NB - 1)
            add_eps(NB - 1)
            invert_deviation(NB - 1)
            normalize(NB - 1, 0)

        @block.tensor
        def _(pe):
            t = nc.tensor
            pe.wait_ge(s_const, CONSTS)
            pe.wait_ge(s_count, NK + 2)
            t.matmul(psum[:, 0, 0:NK], ones_mat, count, start=True, stop=True)
            t.matmul(psum[:, 0, NK:2 * NK], lower, count, start=True, stop=True).then_inc(s_prefix, 1)
            pe.wait_ge(s_start, 1)
            t.transpose(psum[0:NK, 1, 0:P], first_group, ident[:, :]).then_inc(s_startT, 1)
            pe.wait_ge(s_began, 1)
            for h in range(2):
                last = t.matmul(psum[:, 2 + h, 0:GROUPS // 2], ones_mat[0:NK, :],
                                started[0:NK, h * GROUPS // 2:(h + 1) * GROUPS // 2], start=True, stop=True)
            last.then_inc(s_gb, 1)

            with pe.Fori(0, BATCHES // RING) as i:
                for r in range(RING):
                    q = i * RING + r
                    pe.wait_ge(s_xr, q + 1)
                    pe.wait_ge(s_xd, q + 1)
                    for h in range(2):
                        pe.wait_ge(s_added, 2 * q + h + 2 * RING - 3)
                        for z in range(2):
                            for j in range(HALF):
                                last = t.matmul(psum[:, 4 * (r % 2) + 2 * h + z, 0:SUMS_A], hot[r][:, h * HALF + j, :],
                                                feat[r][:, h * HALF + j, z * SUMS_A:(z + 1) * SUMS_A],
                                                start=(j == 0), stop=(j == HALF - 1), skip_group_check=True)
                        last.then_inc(s_grp, 1)

            pe.wait_ge(s_wready, 2)
            pe.wait_ge(s_added, GROUPS + 2 * RING)
            weight_of = [(w_sv01, S, D), (w_lm[:, 0:S], 0, S), (w_wm[:, 0:S], 0, S), (w_lm[:, S:D], S, D), (w_wm[:, S:D], S, D), (w_sv2, 0, D)]
            turned = [(P, 2 * D, 5, 2 * P, 0), (S, 0, 5, 0, P), (S, D, 5, P, 2 * P), (3 * V, S, 4, 0, 3 * P),
                      (3 * V, D + S, 4, P, 4 * P), (3 * V, 2 * D + 2 * S, 4, 2 * P, 5 * P)]

            def turn(b, p):
                pe.wait_ge(s_blk, b + 1)
                for rows, c, bank, to, _ in turned:
                    t.transpose(psum[0:rows, bank, to:to + P], blk_sum[:, c:c + rows], ident[:, :])
                t.transpose(psum[0:S, 5, 3 * P:4 * P], blk_x[p][:, 0:S], ident[:, :])
                t.transpose(psum[0:3 * V, 4, 3 * P:4 * P], blk_x[p][:, S:D], ident[:, :]).then_inc(s_t, 1)

            def messages(b, p):
                pe.wait_ge(s_tt, b + 1)
                for n, (rows, _, _, _, at) in enumerate(turned):
                    w, c0, c1 = weight_of[n]
                    last = t.matmul(psum[:, 6, c0:c1], flip[0:rows, at:at + P], w[0:rows, :],
                                    start=(n == 0), stop=(n == len(turned) - 1), skip_group_check=True)
                last.then_inc(s_ag, 1)

            def turn_a0(b, p):
                pe.wait_ge(s_const, CONSTS)
                pe.wait_ge(s_agc, b + 1)
                t.transpose(psum[0:S, 6, D:D + P], agg[p][:, 0:S], ident[:, :]).then_inc(s_a0, 1)

            def product_s(b, p, *banks):
                for n in banks:
                    pe.wait_ge(s_sfree, b * ZSS + n + 1)
                    t.matmul(psum[:, n % SRING, :], (xs_high if n % 2 else xs_low)[p], w_ss[:, n // 2 * BANK:(n // 2 + 1) * BANK],
                             start=True, stop=True).then_inc(s_zs, 1)

            def product_u(b, p, z):
                n, k = z // 2, z % 2
                if k:
                    pe.wait_ge(s_a0c, b + 1)
                pe.wait_ge(s_ufree, b * 2 * ZU + z + 1)
                t.matmul(psum[:, 2 + z % URING, :], (a0_t if k else xs_low)[p], w_u1[:, n * BANK:(n + 1) * BANK],
                         start=True, stop=True).then_inc(s_zu, 1)

            def turn_gram(b):
                pe.wait_ge(s_g, b * 5 + 5)
                for c in range(8):
                    last = t.transpose(psum[:, 4 + c // 4, c % 4 * P:c % 4 * P + P], gram[:, c * P:(c + 1) * P], ident[:, :])
                    if c % 4 == 3:
                        last.then_inc(s_gt, 1)

            def other_terms(b, p, first=False):
                if not first:
                    pe.wait_ge(s_y, (b - 1) * 4 + 1)
                pe.wait_ge(s_gtc, b * 2 + 3)
                to = psum[:, 7, 0:D]
                t.matmul(to[:, 0:S], xs_low[p][0:S, :], w_lin[0:S, 0:S], start=True, stop=False, skip_group_check=True)
                t.matmul(to[:, S:D], xv_t[p][0:3 * V, :], w_lin[0:3 * V, S:D], start=False, stop=False, skip_group_check=True)
                for c in range(8):
                    last = t.matmul(to[:, 0:S], gram_t[c // 4][:, c % 4 * P:c % 4 * P + P], w_vv[:, c, :],
                                    start=False, stop=(c == 7), skip_group_check=True)
                last.then_inc(s_u, 1)

            def block_(b, p, before=True, after=True, first_before=False):
                product_s(b, p, 0)
                product_u(b, p, 1)
                product_s(b, p, 1)
                if before:
                    turn_gram(b - 1)
                product_s(b, p, 2, 3)
                if before:
                    other_terms(b - 1, 1 - p, first_before)
                product_s(b, p, 4)
                product_u(b, p, 2)
                if after:
                    turn(b + 1, 1 - p)
                product_u(b, p, 3)
                product_s(b, p, 5)
                if after:
                    messages(b + 1, 1 - p)
                product_s(b, p, 6)
                if after:
                    turn_a0(b + 1, 1 - p)
                    product_u(b + 1, 1 - p, 0)
                product_s(b, p, 7)

            turn(0, 0)
            messages(0, 0)
            turn_a0(0, 0)
            product_u(0, 0, 0)
            block_(0, 0, False)
            block_(1, 1, first_before=True)
            with pe.Fori(1, PAIRS_OF_BLOCKS) as i:
                block_(i * 2, 0)
                block_(i * 2 + 1, 1)
            block_(NB - 1, 0, after=False)
            turn_gram(NB - 1)
            other_terms(NB - 1, 0)


_INS = ['x', 'src', 'dst', 'edge_attr_4', 'node_vec1', 'L0_gnn_Wm_ss', 'L0_gnn_Wm_vv', 'L0_gnn_Wm_sv', 'L0_gnn_Wm_vs',
        'L0_gnn_Lm_s', 'L0_gnn_Lm_v', 'L0_gnn_Wu_ss', 'L0_gnn_Wu_vv', 'L0_gnn_Wu_sv', 'L0_gnn_Wu_vs', 'L0_gnn_Lu_s',
        'L0_gnn_Lu_v']


def kernel(**inputs):
    import numpy as _np
    import concourse.bacc as _bacc
    from concourse import mybir as _mybir
    from concourse.bass_utils import run_bass_kernel_spmd as _run

    nc = _bacc.Bacc("TRN2", target_bir_lowering=False, num_devices=1)
    arrays, args = {}, []
    for name in _INS:
        a = _np.ascontiguousarray(inputs[name])
        arrays[f"in_{name}_dram"] = a
        args.append(nc.dram_tensor(f"in_{name}_dram", a.shape, _mybir.dt.from_np(a.dtype), kind="ExternalInput").ap())
    out = nc.dram_tensor("out_0_dram", inputs['x'].shape, _mybir.dt.float32, kind="ExternalOutput").ap()
    gnn_kernel(nc, *args, out)
    r = _run(nc, [arrays], core_ids=[0])
    return r.results[0]["out_0_dram"]
```
